# Optimizing a Trainium2 kernel written in Bass

```python
import numpy as np
import jax
import jax.numpy as jnp

def _softmax(x, axis=-1):
    return jax.nn.softmax(x, axis=axis)

def _gelu(x):
    return jax.nn.gelu(x, approximate=True)

def _silu(x):
    return jax.nn.silu(x)

def _sigmoid(x):
    return jax.nn.sigmoid(x)

def _layernorm(x, axis=-1, eps=1e-05):
    m = jnp.mean(x, axis=axis, keepdims=True)
    v = jnp.var(x, axis=axis, keepdims=True)
    return (x - m) / jnp.sqrt(v + eps)

def _scatter_add(tgt, idx, src, axis=0):
    return tgt.at[idx].add(src)

def _segment_sum(src, seg, n):
    return jax.ops.segment_sum(src, seg, n)
kernel_name = 'mk_seq_postln_d1_jaxref_r4_d46044'

def setup_inputs(seed: int=0):
    np.random.seed(seed)
    _w = jnp.asarray

    def _L0_attn_setup():
        import jax, jax.numpy as jnp
        import numpy as np
        B, N, D, H = (2, 512, 256, 8)
        HD = D // H
        EPS = 1e-06

        def _interleave(a, b):
            return jnp.stack([a, b], axis=2).reshape(a.shape[0], 2 * a.shape[1], a.shape[2], a.shape[3])

        def _l2norm(x):
            return x / jnp.sqrt(jnp.sum(x * x, axis=-1, keepdims=True) + EPS)

        def _dense_rnn(x, Wq, Wk, Wv, Wf1, Wf2, Wbeta, Wog1, Wog2, norm_w, Wo):
            b, n, d = x.shape
            q = jax.nn.silu(x @ Wq)
            k = jax.nn.silu(x @ Wk)
            v = jax.nn.silu(x @ Wv)
            f = x @ Wf1 @ Wf2
            log_f = jax.nn.log_sigmoid(f)
            beta = jax.nn.sigmoid(x @ Wbeta) * 2.0
            shp = (b, n, H, HD)
            q, k, v, log_f = (t.reshape(shp) for t in (q, k, v, log_f))
            k = _l2norm(k)
            k_ = -beta[..., None] * k
            zero = jnp.zeros(shp, x.dtype)
            gk = _interleave(log_f, zero)
            a = _interleave(k_ * jnp.exp(log_f), k_)
            bb = _interleave(k, k)
            kk = _interleave(zero, k)
            vv = _interleave(zero, v)
            qq = _interleave(zero, q)
            seq = tuple((jnp.moveaxis(t, 1, 0) for t in (gk, a, bb, kk, vv, qq)))
            S0 = jnp.zeros((b, H, HD, HD), x.dtype)

            def step(S, inp):
                g, a_t, b_t, k_t, v_t, q_t = inp
                bS = jnp.einsum('bhk,bhkv->bhv', b_t, S)
                S = jnp.exp(g)[..., None] * S + a_t[..., None] * bS[:, :, None, :] + k_t[..., None] * v_t[:, :, None, :]
                o = jnp.einsum('bhk,bhkv->bhv', q_t, S)
                return (S, o)
            _, o = jax.lax.scan(step, S0, seq)
            o = jnp.moveaxis(o, 0, 1)[:, 1::2]
            out = o.reshape(b, n, d)
            gate = x @ Wog1 @ Wog2
            y = out * jax.nn.sigmoid(gate)
            yh = y.reshape(b, n, H, HD)
            yh = yh / jnp.sqrt(jnp.mean(yh * yh, axis=-1, keepdims=True) + EPS)
            y = yh.reshape(b, n, d) * norm_w
            return y @ Wo
        key = jax.random.key(seed)
        ks = jax.random.split(key, 11)
        std = 0.02
        w = lambda k, shape: jax.random.normal(k, shape, dtype=jnp.float32) * std
        return {'x': jax.random.normal(ks[0], (B, N, D), dtype=jnp.float32), 'Wq': w(ks[1], (D, D)), 'Wk': w(ks[2], (D, D)), 'Wv': w(ks[3], (D, D)), 'Wf1': w(ks[4], (D, HD)), 'Wf2': w(ks[5], (HD, D)), 'Wbeta': w(ks[6], (D, H)), 'Wog1': w(ks[7], (D, HD)), 'Wog2': w(ks[8], (HD, D)), 'norm_w': jnp.ones((D,), dtype=jnp.float32), 'Wo': w(ks[9], (D, D))}
    _L0_attn_in = _L0_attn_setup()

    def _L0_ffn_setup():
        import jax, jax.numpy as jnp
        import numpy as np
        ALPHA = 1.0
        key = jax.random.key(seed)
        ks = jax.random.split(key, 7)
        B, S, IN, OUT = (8, 2048, 256, 256)
        RANK, DDIM, UDIM = (4, 100, 50)
        return {'hidden_states': jax.random.normal(ks[0], (B, S, IN), dtype=jnp.float32), 'W': jax.random.normal(ks[1], (OUT, IN), dtype=jnp.float32) * 0.02, 'b': jax.random.normal(ks[2], (OUT,), dtype=jnp.float32) * 0.02, 'lora_down': jax.random.normal(ks[3], (RANK, DDIM), dtype=jnp.float32) * 0.1, 'lora_up': jax.random.normal(ks[4], (UDIM, RANK), dtype=jnp.float32) * 0.1, 'down_aux': jax.random.normal(ks[5], (DDIM, IN), dtype=jnp.float32) * 0.03, 'up_aux': jax.random.normal(ks[6], (OUT, UDIM), dtype=jnp.float32) * 0.03}
    _L0_ffn_in = _L0_ffn_setup()
    _d = {'L0_attn_x': _L0_attn_in['x'], 'L0_attn_Wq': _L0_attn_in['Wq'], 'L0_attn_Wk': _L0_attn_in['Wk'], 'L0_attn_Wv': _L0_attn_in['Wv'], 'L0_attn_Wf1': _L0_attn_in['Wf1'], 'L0_attn_Wf2': _L0_attn_in['Wf2'], 'L0_attn_Wbeta': _L0_attn_in['Wbeta'], 'L0_attn_Wog1': _L0_attn_in['Wog1'], 'L0_attn_Wog2': _L0_attn_in['Wog2'], 'L0_attn_norm_w': _L0_attn_in['norm_w'], 'L0_attn_Wo': _L0_attn_in['Wo'], 'L0_ffn_W': _L0_ffn_in['W'], 'L0_ffn_b': _L0_ffn_in['b'], 'L0_ffn_lora_down': _L0_ffn_in['lora_down'], 'L0_ffn_lora_up': _L0_ffn_in['lora_up'], 'L0_ffn_down_aux': _L0_ffn_in['down_aux'], 'L0_ffn_up_aux': _L0_ffn_in['up_aux']}
    _x0 = _d['L0_attn_x']
    _d['L0_attn_x'] = jax.random.normal(jax.random.fold_in(jax.random.key(seed), 1), (32, 512, 256), dtype=_x0.dtype)
    del _x0
    return _d

def reference(L0_attn_x, L0_attn_Wq, L0_attn_Wk, L0_attn_Wv, L0_attn_Wf1, L0_attn_Wf2, L0_attn_Wbeta, L0_attn_Wog1, L0_attn_Wog2, L0_attn_norm_w, L0_attn_Wo, L0_ffn_W, L0_ffn_b, L0_ffn_lora_down, L0_ffn_lora_up, L0_ffn_down_aux, L0_ffn_up_aux):

    def _L0_attn_ref(x, Wq, Wk, Wv, Wf1, Wf2, Wbeta, Wog1, Wog2, norm_w, Wo):
        import jax, jax.numpy as jnp
        import numpy as np
        B, N, D, H = (2, 512, 256, 8)
        HD = D // H
        EPS = 1e-06

        def _interleave(a, b):
            return jnp.stack([a, b], axis=2).reshape(a.shape[0], 2 * a.shape[1], a.shape[2], a.shape[3])

        def _l2norm(x):
            return x / jnp.sqrt(jnp.sum(x * x, axis=-1, keepdims=True) + EPS)

        def _dense_rnn(x, Wq, Wk, Wv, Wf1, Wf2, Wbeta, Wog1, Wog2, norm_w, Wo):
            b, n, d = x.shape
            q = jax.nn.silu(x @ Wq)
            k = jax.nn.silu(x @ Wk)
            v = jax.nn.silu(x @ Wv)
            f = x @ Wf1 @ Wf2
            log_f = jax.nn.log_sigmoid(f)
            beta = jax.nn.sigmoid(x @ Wbeta) * 2.0
            shp = (b, n, H, HD)
            q, k, v, log_f = (t.reshape(shp) for t in (q, k, v, log_f))
            k = _l2norm(k)
            k_ = -beta[..., None] * k
            zero = jnp.zeros(shp, x.dtype)
            gk = _interleave(log_f, zero)
            a = _interleave(k_ * jnp.exp(log_f), k_)
            bb = _interleave(k, k)
            kk = _interleave(zero, k)
            vv = _interleave(zero, v)
            qq = _interleave(zero, q)
            seq = tuple((jnp.moveaxis(t, 1, 0) for t in (gk, a, bb, kk, vv, qq)))
            S0 = jnp.zeros((b, H, HD, HD), x.dtype)

            def step(S, inp):
                g, a_t, b_t, k_t, v_t, q_t = inp
                bS = jnp.einsum('bhk,bhkv->bhv', b_t, S)
                S = jnp.exp(g)[..., None] * S + a_t[..., None] * bS[:, :, None, :] + k_t[..., None] * v_t[:, :, None, :]
                o = jnp.einsum('bhk,bhkv->bhv', q_t, S)
                return (S, o)
            _, o = jax.lax.scan(step, S0, seq)
            o = jnp.moveaxis(o, 0, 1)[:, 1::2]
            out = o.reshape(b, n, d)
            gate = x @ Wog1 @ Wog2
            y = out * jax.nn.sigmoid(gate)
            yh = y.reshape(b, n, H, HD)
            yh = yh / jnp.sqrt(jnp.mean(yh * yh, axis=-1, keepdims=True) + EPS)
            y = yh.reshape(b, n, d) * norm_w
            return y @ Wo
        return _dense_rnn(x, Wq, Wk, Wv, Wf1, Wf2, Wbeta, Wog1, Wog2, norm_w, Wo)

    def _L0_ffn_ref(hidden_states, W, b, lora_down, lora_up, down_aux, up_aux):
        import jax, jax.numpy as jnp
        import numpy as np
        ALPHA = 1.0
        lilora_weight = up_aux @ (lora_up @ (lora_down @ down_aux))
        base = jnp.einsum('bsi,oi->bso', hidden_states, W) + b
        delta = jnp.einsum('bsi,oi->bso', hidden_states, lilora_weight)
        return base + ALPHA * delta
    x = L0_attn_x
    x = _layernorm(x + _L0_attn_ref(x, L0_attn_Wq, L0_attn_Wk, L0_attn_Wv, L0_attn_Wf1, L0_attn_Wf2, L0_attn_Wbeta, L0_attn_Wog1, L0_attn_Wog2, L0_attn_norm_w, L0_attn_Wo), axis=-1)
    x = _layernorm(x + _L0_ffn_ref(x, L0_ffn_W, L0_ffn_b, L0_ffn_lora_down, L0_ffn_lora_up, L0_ffn_down_aux, L0_ffn_up_aux), axis=-1)
    return x

_drawn_inputs = setup_inputs


def setup_inputs(seed=0):
    import zlib

    import numpy as np

    out = dict(_drawn_inputs(seed))
    spreads = {'L0_attn_norm_w': (1.0, 0.2)}
    factors = {'L0_attn_Wf1': 8.0,
     'L0_attn_Wf2': 8.0,
     'L0_attn_Wbeta': 8.0,
     'L0_attn_Wog1': 8.0,
     'L0_attn_Wog2': 8.0,
     'L0_ffn_b': 2.921,
     'L0_ffn_lora_down': 2.957,
     'L0_ffn_lora_up': 3.34,
     'L0_ffn_down_aux': 3.099,
     'L0_ffn_up_aux': 3.086}
    for name, (base, spread) in spreads.items():
        noise = np.random.default_rng([zlib.crc32(name.encode()), seed]).standard_normal(out[name].shape)
        drawn = base * np.exp(spread * noise) if base else spread * noise
        out[name] = jnp.asarray(drawn.astype(out[name].dtype))
    for name, factor in factors.items():
        out[name] = (out[name] * factor).astype(out[name].dtype)
    return out
```

```python
from contextlib import ExitStack

import numpy as np

import concourse.bass as bass
from concourse import mybir

ALU = mybir.AluOpType
ACT = mybir.ActivationFunctionType
F32 = mybir.dt.float32
I32 = mybir.dt.int32

P = 128
H, HD = 8, 32
D = H * HD
HF = D // P
HPH = P // HD
GB = 2
TB = 8
STEPS = 2
ROWS = TB * STEPS
BANK = 512
L2_EPS = 1e-6
RMS_EPS = 1e-6
LN_EPS = 1e-5
MIN_DECAY = 2.0 ** -24

C_IDENT = 0
C_HEADS = C_IDENT + P
C_EXPAND = C_HEADS + P
C_BATCH = C_EXPAND + D
C_HALF = C_BATCH + GB
C_EYE = C_HALF + GB * HD
C_EPS = C_EYE + ROWS * ROWS
C_END = C_EPS + 2
M_LOW = 0
M_Q = M_LOW + GB * ROWS
M_END = M_Q + GB * TB


def constants():
    f = np.zeros((P, C_END), np.float32)
    p = np.arange(P)
    f[:, C_IDENT:C_IDENT + P] = np.eye(P)
    f[:, C_HEADS:C_HEADS + P] = p[:, None] // HD == p[None] // HD
    for h in range(H):
        f[2 * HD + h, C_EXPAND + h * HD:C_EXPAND + (h + 1) * HD] = 1
    batch = p % HD // ROWS
    for b in range(GB):
        f[:, C_BATCH + b] = batch == b
        f[:, C_HALF + b * HD:C_HALF + (b + 1) * HD] = (batch == b)[:, None]
    f[:, C_EYE:C_EYE + ROWS * ROWS] = np.eye(ROWS).ravel()
    f[:, C_EPS] = L2_EPS
    f[:, C_EPS + 1] = LN_EPS
    m = np.zeros((P, M_END), np.int32)
    row = p % ROWS
    for b in range(GB):
        m[:, M_LOW + b * ROWS:M_LOW + (b + 1) * ROWS] = (batch == b)[:, None] & (row[:, None] < np.arange(ROWS))
        m[:, M_Q + b * TB:M_Q + (b + 1) * TB] = (batch == b)[:, None] & (row[:, None] // STEPS <= np.arange(TB))
    return f, m


class Signal:

    def __init__(self, handle, each, primed=False):
        self.handle, self.each, self.primed = handle, each, primed
        self.base = each if primed else 0

    def wait(self, engine, g, count):
        assert 0 < count <= self.each
        engine.wait_ge(self.handle, g * self.each + (self.base + count))

    def wait_previous(self, engine, g):
        assert self.primed
        engine.wait_ge(self.handle, g * self.each + self.base)


def delta_block(nc, x, xt, wq, wk, wv, wf1, wf2, wbeta, wog1, wog2, norm_w, wo, ffn_wt, ffn_b,
                lora_down_t, lora_up_t, down_aux, up_aux_t, const_f, const_i, out):
    NB, NT, _ = x.shape
    G = NB // GB
    TOK = GB * NT
    NBLK = NT // TB
    TILES = HF * NBLK
    assert TILES == P and NT == BANK and GB * ROWS == HD
    TT = TOK // P
    KT = D // P
    SLOTS = TB + 1
    SMALL = 2 * HD + H
    RANK, DD = lora_down_t.shape[1], lora_down_t.shape[0]
    UD = up_aux_t.shape[0]

    STAGES = [("small", GB), ("proj", 6 * GB * HF), ("kss", GB * HF), ("a", TILES // 8), ("nt", 8), ("tt", 4),
              ("xu", TILES // 16), ("yss", GB * HF), ("wo", TT // 2), ("ht", TT // 2), ("ff", TT // 2)]
    RING = 3
    FILLS = [(s, i) for s, n in STAGES for i in range(n)]
    AT = {f: n for n, f in enumerate(FILLS)}
    US_BANKS, S_BANK, O_BANKS = (3, 4), 5, (6, 7)
    OSTEPS = BANK // (HF * GB * TB)
    NO = NBLK // OSTEPS

    with ExitStack() as ctx:
        def sb(name, shape, dt=F32):
            return ctx.enter_context(nc.sbuf_tensor(name, shape, dt))

        def signal(name, each, primed=False):
            made = Signal(ctx.enter_context(nc.semaphore(name)), each, primed)
            if primed:
                primed_signals.append(made)
            return made

        primed_signals = []

        w_kqv = sb("w_kqv", [P, KT, 3, D])
        w_small = sb("w_small", [P, KT, SMALL])
        w_second = sb("w_second", [P, D])
        w_out = sb("w_out", [P, HF, D])
        w_ffn = sb("w_ffn", [P, KT, D])
        bias_row = sb("bias_row", [P, D])
        norm_col = sb("norm_col", [P, HF])
        cf = sb("cf", [P, C_END])
        ci = sb("ci", [P, M_END], I32)
        x_col = sb("x_col", [P, KT, TOK])
        scratch = sb("scratch", [P, 4, HF * TOK])
        logf = sb("logf", [P, HF, GB, NBLK, SLOTS])
        dd = sb("dd", [P, HF * GB * NBLK * SLOTS])
        epm = sb("epm", [P, 2, HF * GB * NBLK * SLOTS])
        uq = sb("uq", [P, TILES, HD + GB * TB])
        w_col = sb("w_col", [P, TILES, HD])
        v_col = sb("v_col", [P, TILES, HD])
        gate = sb("gate", [P, HF, TOK])
        edge = sb("edge", [P, HF, NBLK, GB])
        w_row = sb("w_row", [P, TILES, HD])
        v_row = sb("v_row", [P, TILES, HD])
        aq = sb("aq", [P, TILES, GB * TB])
        prod = sb("prod", [P, GB * HPH * ROWS * ROWS // 4])
        state = sb("state", [P, HF, GB, HD])
        moved = sb("moved", [P, HF, GB, HD])
        delta = sb("delta", [P, HF, GB, HD])
        stats = sb("stats", [P, TT, 6])
        mean_var = sb("mean_var", [P, TT, 2])
        rstd = sb("rstd", [P, TT])
        lora_a = sb("lora_a", [RANK, D])
        lora_b = sb("lora_b", [UD, D])
        k_col, q_col, beta_col, ss_col = (scratch[:, i, :].rearrange("p (f t) -> p f t", f=HF) for i in range(4))
        u_row = scratch[:, 0:2, :].rearrange("p a (t c) -> p (a t) c", c=HD)
        low = scratch[:, 2, :]
        inv = scratch[:, 3, :]
        y_col, r_col = k_col, q_col
        h_col = beta_col
        h_row = scratch[:, 3, :].rearrange("p (t c) -> p t c", c=D)
        small = dd[:, 0:TOK]
        dd4 = dd[:, :].rearrange("p (f b n s) -> p f b n s", f=HF, b=GB, s=SLOTS)
        ep, em = (epm[:, i, :].rearrange("p (f b n s) -> p f b n s", f=HF, b=GB, s=SLOTS) for i in range(2))
        o_col = dd[:, 0:HF * TOK].rearrange("p (f t) -> p f t", f=HF)
        flat = epm[:, :, :].rearrange("p a b -> p (a b)")
        a_t = flat[:, 0:TILES * HD].rearrange("p (m i) -> p m i", i=HD)
        xu_t = a_t
        t_t = w_col
        lora_d = x_col[0:DD, 0, 0:RANK]
        lora_u = x_col[0:RANK, 0, RANK:RANK + UD]
        aux_d = x_col[0:DD, 0, 256:256 + D]
        aux_u = x_col[0:UD, 0, 512:512 + D]

        ident = cf[:, C_IDENT:C_IDENT + P]
        same_head = cf[:, C_HEADS:C_HEADS + P]

        psum = [ctx.enter_context(nc.psum_tensor(f"bank{i}", [P, BANK], F32)) for i in range(8)]

        def bank(stage, i):
            return psum[AT[(stage, i)] % RING]

        weights_in = signal("weights_in", 0)
        lora_step = signal("lora_step", 0)
        lora_copied = signal("lora_copied", 0)
        set_up = signal("set_up", 0)
        x_col_in = signal("x_col_in", 16)
        x_row_in = signal("x_row_in", 16)
        out_stored = signal("out_stored", 16, primed=True)
        filled = {s: signal(f"{s}_filled", n, primed=s in ("proj", "ff")) for s, n in STAGES}
        drained = {s: signal(f"{s}_drained", n, primed=s == STAGES[-1][0]) for s, n in STAGES}
        k_squared = signal("k_squared", GB * HF)
        f_floored = signal("f_floored", GB * HF)
        f_logged = signal("f_logged", GB * HF)
        r_ready = signal("r_ready", GB * HF)
        k_normed = signal("k_normed", GB * HF)
        kb_ready = signal("kb_ready", GB * HF)
        carry_set = signal("carry_set", 2)
        summed = signal("summed", HF)
        centred = signal("centred", GB * HF)
        ep_ready = signal("ep_ready", HF)
        em_ready = signal("em_ready", HF)
        u_ready = signal("u_ready", GB * HF * STEPS)
        w_ready = signal("w_ready", GB * HF * STEPS)
        q_ready = signal("q_ready", GB * HF)
        edge_ready = signal("edge_ready", GB * HF)
        rows_turned = signal("rows_turned", 3 * HF)
        a_cleared = signal("a_cleared", 1)
        solve_step = signal("solve_step", 1 + 2 * (ROWS - 1))
        us_filled = signal("us_filled", NBLK)
        delta_ready = signal("delta_ready", NBLK)
        s_filled = signal("s_filled", NBLK - 1)
        moved_ready = signal("moved_ready", NBLK - 1)
        state_ready = signal("state_ready", NBLK)
        o_filled = signal("o_filled", NO)
        o_copied = signal("o_copied", NO * HF, primed=True)
        y_ready = signal("y_ready", GB * HF)
        y_squared = signal("y_squared", GB * HF)
        yr_ready = signal("yr_ready", GB * HF)
        y_normed = signal("y_normed", GB * HF)
        stats_ready = signal("stats_ready", 2 * TT)
        mean_ready = signal("mean_ready", 2 * TT)
        var_logged = signal("var_logged", 2)
        rstd_ready = signal("rstd_ready", 2)
        h_normed = signal("h_normed", 2 * TT)
        bias_added = signal("bias_added", TT)

        halves = [(b, f) for b in range(GB) for f in range(HF)]

        def tokens(b):
            return slice(b * NT, (b + 1) * NT)

        def blocks(col, b, f):
            return col[:, f, tokens(b)].rearrange("p (n t) -> p n t", t=TB)

        def tiles(f):
            return slice(f * NBLK, (f + 1) * NBLK)

        def quarter(h):
            return slice(h * HD, (h + 1) * HD)

        n_weights = 0
        block = ctx.enter_context(nc.Block())

        wait_registers = {e.engine: [e.alloc_register(f"until{i}") for i in range(4)]
                          for e in (nc.tensor, nc.vector, nc.gpsimd)}

        def wait_apart(engine, g, *waits):
            values = []
            for (s, count), reg in zip(waits, wait_registers[engine.engine]):
                engine.reg_alu(reg, g, s.each, ALU.mult)
                engine.reg_add(reg, reg, s.base + count)
                values.append(engine.snap(reg))
            engine.wait_ge(set_up.handle, 4)
            for (s, _), v in zip(waits, values):
                engine.wait_ge(s.handle, v)

        loads = [(w_kqv[:, :, 0, :], wk.rearrange("(a p) n -> p a n", p=P)),
                 (w_kqv[:, :, 1, :], wq.rearrange("(a p) n -> p a n", p=P)),
                 (w_kqv[:, :, 2, :], wv.rearrange("(a p) n -> p a n", p=P)),
                 (w_small[:, :, 0:HD], wf1.rearrange("(a p) n -> p a n", p=P)),
                 (w_small[:, :, HD:2 * HD], wog1.rearrange("(a p) n -> p a n", p=P)),
                 (w_small[:, :, 2 * HD:SMALL], wbeta.rearrange("(a p) n -> p a n", p=P)),
                 (w_second[0:HD, :], wf2), (w_second[HD:2 * HD, :], wog2),
                 (w_second[2 * HD:SMALL, :], const_f[2 * HD:SMALL, C_EXPAND:C_EXPAND + D]),
                 (w_out[:, :, :], wo.rearrange("(a p) n -> p a n", p=P)),
                 (w_ffn[:, :, :], ffn_wt.rearrange("(a p) n -> p a n", p=P)),
                 (bias_row[:, :], ffn_b.rearrange("(a n) -> a n", a=1).to_broadcast([P, D])),
                 (norm_col[:, :], norm_w),
                 (cf[:, :], const_f), (ci[:, :], const_i),
                 (lora_d, lora_down_t), (lora_u, lora_up_t), (aux_d, down_aux), (aux_u, up_aux_t)]
        n_weights = 16 * len(loads)

        @block.sync
        def _(sp):
            for dst, src in loads:
                sp.dma_start(dst, src).then_inc(weights_in.handle, 16)
            sp.wait_ge(lora_step.handle, 4)
            xt_view = xt.rearrange("(a p) t -> p a t", p=P)
            rows = x.rearrange("b t d -> (b t) d").rearrange("(n p) d -> p n d", p=P)
            out_rows = out.rearrange("b t d -> (b t) d").rearrange("(n p) d -> p n d", p=P)
            with sp.Fori(0, G) as g:
                filled["proj"].wait_previous(sp, g)
                sp.dma_start(x_col[:, :, :], xt_view[:, :, bass.ds(g * TOK, TOK)]).then_inc(x_col_in.handle, 16)
                filled["tt"].wait(sp, g, 4)
                sp.dma_start(h_row, rows[:, bass.ds(g * TT, TT), :]).then_inc(x_row_in.handle, 16)
                h_normed.wait(sp, g, 2 * TT)
                sp.dma_start(out_rows[:, bass.ds(g * TT, TT), :], h_row).then_inc(out_stored.handle, 16)
            sp.wait_ge(out_stored.handle, out_stored.base + 16 * G)

        @block.gpsimd
        def _(pool):
            pool.memset(v_col[:, :, :], 0.0).then_inc(set_up.handle, 1)
            pool.memset(logf[:, :, :, :, :], 0.0).then_inc(set_up.handle, 1)
            pool.memset(aq[:, :, :], 0.0).then_inc(set_up.handle, 1)
            for s in primed_signals:
                pool.sem_inc(s.handle, s.each)
            pool.sem_inc(set_up.handle, 1)
            pool.wait_ge(weights_in.handle, n_weights)
            with pool.Fori(0, G) as g:
                for i, (b, f) in enumerate(halves):
                    drained["proj"].wait(pool, g, 2 * GB * HF)
                    ep_ready.wait(pool, g, f + 1)
                    pool.tensor_tensor(
                        uq[:, tiles(f), HD + b * TB:HD + (b + 1) * TB], blocks(q_col, b, f),
                        ep[:, f, b, :, 1:SLOTS], ALU.mult).then_inc(q_ready.handle, 1)
                for i, (b, f) in enumerate(halves):
                    k_normed.wait(pool, g, i + 1)
                    em_ready.wait(pool, g, f + 1)
                    for s in range(STEPS):
                        pool.tensor_tensor(
                            w_col[:, tiles(f), b * ROWS + s:(b + 1) * ROWS:STEPS], blocks(k_col, b, f),
                            em[:, f, b, :, s:s + TB], ALU.mult).then_inc(w_ready.handle, 1)
                    pool.tensor_tensor(
                        edge[:, f, 0:NBLK - 1, b], ep[:, f, b, 0:NBLK - 1, TB],
                        em[:, f, b, 1:NBLK, 0], ALU.mult).then_inc(edge_ready.handle, 1)
                wait_apart(pool, g, (u_ready, GB * HF * STEPS), (w_ready, GB * HF * STEPS), (edge_ready, GB * HF))
                pool.memset(a_t, 0.0).then_inc(a_cleared.handle, 1)
                for t in range(TT):
                    if t % 2 == 0:
                        filled["ht"].wait(pool, g, t // 2 + 1)
                    pool.tensor_tensor(h_row[:, t, :], h_row[:, t, :], bias_row[:, :],
                                       ALU.add).then_inc(bias_added.handle, 1)

        @block.tensor
        def _(pe):
            pe.wait_ge(weights_in.handle, n_weights)
            pe.matmul(psum[0][0:RANK, 0:D], lora_d, aux_d, start=True, stop=True).then_inc(lora_step.handle, 1)
            pe.wait_ge(lora_copied.handle, 1)
            pe.matmul(psum[1][0:UD, 0:D], lora_u, lora_a[:, :], start=True, stop=True).then_inc(lora_step.handle, 1)
            pe.wait_ge(lora_copied.handle, 2)
            for a in range(KT):
                pe.matmul(psum[2][:, a * D:(a + 1) * D] if KT * D <= BANK else None, lora_b[:, a * P:(a + 1) * P],
                          aux_u, start=True, stop=True).then_inc(lora_step.handle, 1)
            pe.wait_ge(lora_copied.handle, 2 + KT)

            def last_read(stage, i):
                n = AT[(stage, i)]
                s, j = FILLS[n - RING]
                return drained[s], j + 1 if n >= RING else 0

            def claim(g, stage, i):
                s, count = last_read(stage, i)
                pe.wait_ge(s.handle, g * s.each + (s.base + count))
                assert s.base + count > 0
                return bank(stage, i)

            with pe.Fori(0, G) as g:
                x_col_in.wait(pe, g, 16)
                for b in range(GB):
                    ps = claim(g, "small", b)
                    for a in range(KT):
                        mm = pe.matmul(ps[0:SMALL, :], w_small[:, a, :], x_col[:, a, tokens(b)],
                                       start=a == 0, stop=a == KT - 1)
                    mm.then_inc(filled["small"].handle, 1)
                i = 0
                for w in range(3):
                    for b, f in halves:
                        ps = claim(g, "proj", i)
                        for a in range(KT):
                            mm = pe.matmul(ps[:, :], w_kqv[:, a, w, f * P:(f + 1) * P], x_col[:, a, tokens(b)],
                                           start=a == 0, stop=a == KT - 1)
                        mm.then_inc(filled["proj"].handle, 1)
                        i += 1
                drained["small"].wait(pe, g, GB)
                for lo, hi in ((0, HD), (2 * HD, SMALL), (HD, 2 * HD)):
                    for b, f in halves:
                        ps = claim(g, "proj", i)
                        pe.matmul(ps[:, :], w_second[lo:hi, f * P:(f + 1) * P], small[lo:hi, tokens(b)],
                                  start=True, stop=True).then_inc(filled["proj"].handle, 1)
                        i += 1
                for i, (b, f) in enumerate(halves):
                    ps = claim(g, "kss", i)
                    k_squared.wait(pe, g, i + 1)
                    pe.matmul(ps[:, :], same_head, ss_col[:, f, tokens(b)], start=True,
                              stop=True).then_inc(filled["kss"].handle, 1)
                for i in range(TILES // 8):
                    inputs = ((w_ready, GB * HF * STEPS), (u_ready, GB * HF * STEPS), (q_ready, GB * HF))
                    wait_apart(pe, g, last_read("a", i), *(inputs if i == 0 else ()))
                    ps = bank("a", i)
                    for j in range(8):
                        m = 8 * i + j
                        for h in range(HPH):
                            mm = pe.matmul(ps[quarter(h), j * 48:(j + 1) * 48], w_col[quarter(h), m, :],
                                           uq[quarter(h), m, :], start=True, stop=True)
                    mm.then_inc(filled["a"].handle, 1)
                drained["a"].wait(pe, g, TILES // 8)
                for i in range(8):
                    ps = claim(g, "nt", i)
                    for j in range(4):
                        mm = pe.transpose(ps[:, j * P:(j + 1) * P], a_t[:, :, 4 * i + j], ident)
                    mm.then_inc(filled["nt"].handle, 1)
                solve_step.wait(pe, g, 1 + 2 * (ROWS - 1))
                for i in range(4):
                    ps = claim(g, "tt", i)
                    for j in range(4):
                        mm = pe.transpose(ps[:, j * P:(j + 1) * P], inv[:, (4 * i + j) * P:(4 * i + j + 1) * P], ident)
                    mm.then_inc(filled["tt"].handle, 1)
                for i in range(TILES // 16):
                    inputs = ((drained["tt"], 4), (rows_turned, 3 * HF))
                    wait_apart(pe, g, last_read("xu", i), *(inputs if i == 0 else ()))
                    ps = bank("xu", i)
                    for j in range(16):
                        m = 16 * i + j
                        for h in range(HPH):
                            mm = pe.matmul(ps[quarter(h), j * HD:(j + 1) * HD], u_row[quarter(h), m, :],
                                           t_t[quarter(h), m, :], start=True, stop=True)
                    mm.then_inc(filled["xu"].handle, 1)

                def us_bank(n):
                    return psum[US_BANKS[n % 2]][:, 0:HF * GB * HD].rearrange("p (f v) -> p f v", f=HF)

                def t_times_v(n):
                    for f in range(HF):
                        for h in range(HPH):
                            v = v_row[quarter(h), f * NBLK + n, :].unsqueeze(1).to_broadcast([HD, GB, HD])
                            pe.matmul(us_bank(n)[quarter(h), f, :], t_t[quarter(h), f * NBLK + n, :], v,
                                      start=f == 0, stop=False, skip_group_check=True)

                wait_apart(pe, g, (drained["xu"], TILES // 16))
                t_times_v(0)
                for n in range(NBLK):
                    o_bank = psum[O_BANKS[n // OSTEPS % 2]]

                    def o_at(f, b):
                        at = ((n % OSTEPS * HF + f) * GB + b) * TB
                        return slice(at, at + TB)

                    wait_apart(pe, g, (state_ready, n + 1))
                    for f in range(HF):
                        for h in range(HPH):
                            mm = pe.matmul(us_bank(n)[quarter(h), f, :], xu_t[quarter(h), f * NBLK + n, :],
                                           state[quarter(h), f, :, :], start=False, stop=True,
                                           skip_group_check=True)
                    mm.then_inc(us_filled.handle, 1)
                    if n % OSTEPS == 0:
                        wait_apart(pe, g, (o_copied, max(0, n // OSTEPS - 1) * HF))
                    for f in range(HF):
                        for b in range(GB):
                            for h in range(HPH):
                                pe.matmul(o_bank[quarter(h), o_at(f, b)], state[quarter(h), f, b, :],
                                          uq[quarter(h), f * NBLK + n, HD + b * TB:HD + (b + 1) * TB],
                                          start=n % OSTEPS == 0 and f == 0 and b == 0, stop=False,
                                          skip_group_check=True)
                    wait_apart(pe, g, (delta_ready, n + 1))
                    if n < NBLK - 1:
                        for f in range(HF):
                            for h in range(HPH):
                                mm = pe.matmul(psum[S_BANK][quarter(h), f * GB * HD:(f + 1) * GB * HD],
                                               w_row[quarter(h), f * NBLK + n, :], delta[quarter(h), f, :, :],
                                               start=True, stop=True)
                        mm.then_inc(s_filled.handle, 1)
                    for f in range(HF):
                        for b in range(GB):
                            for h in range(HPH):
                                mm = pe.matmul(o_bank[quarter(h), o_at(f, b)], delta[quarter(h), f, b, :],
                                               aq[quarter(h), f * NBLK + n, b * TB:(b + 1) * TB],
                                               start=False, stop=True, skip_group_check=True)
                    if n % OSTEPS == OSTEPS - 1:
                        mm.then_inc(o_filled.handle, 1)
                    if n < NBLK - 1:
                        t_times_v(n + 1)

                for i, (b, f) in enumerate(halves):
                    ps = claim(g, "yss", i)
                    y_squared.wait(pe, g, i + 1)
                    pe.matmul(ps[:, :], same_head, r_col[:, f, tokens(b)], start=True,
                              stop=True).then_inc(filled["yss"].handle, 1)
                for i in range(TT // 2):
                    ps = claim(g, "wo", i)
                    y_normed.wait(pe, g, HF * (2 * i * P // NT + 1))
                    for j in range(2):
                        t = 2 * i + j
                        for f in range(HF):
                            mm = pe.matmul(ps[:, j * D:(j + 1) * D], y_col[:, f, t * P:(t + 1) * P], w_out[:, f, :],
                                           start=f == 0, stop=f == HF - 1)
                    mm.then_inc(filled["wo"].handle, 1)
                for i in range(TT // 2):
                    ps = claim(g, "ht", i)
                    h_normed.wait(pe, g, 2 * i + 2)
                    for a in range(KT):
                        for j in range(2):
                            at = (a * 2 + j) * P
                            mm = pe.transpose(ps[:, at:at + P], h_row[:, 2 * i + j, a * P:(a + 1) * P], ident)
                    mm.then_inc(filled["ht"].handle, 1)
                for i in range(TT // 2):
                    ps = claim(g, "ff", i)
                    drained["ht"].wait(pe, g, i + 1)
                    for j in range(2):
                        t = 2 * i + j
                        for a in range(KT):
                            mm = pe.matmul(ps[:, j * D:(j + 1) * D], h_col[:, a, t * P:(t + 1) * P], w_ffn[:, a, :],
                                           start=a == 0, stop=a == KT - 1)
                    mm.then_inc(filled["ff"].handle, 1)

        @block.scalar
        def _(act):
            act.wait_ge(weights_in.handle, n_weights)
            act.wait_ge(set_up.handle, 4)
            eps2 = cf[:, C_EPS:C_EPS + 1]
            eps_ln = cf[:, C_EPS + 1:C_EPS + 2]
            with act.Fori(0, G) as g:
                filled["ff"].wait_previous(act, g)
                i = 0
                for w, dst in enumerate((k_col, q_col, None)):
                    for b, f in halves:
                        filled["proj"].wait(act, g, i + 1)
                        ps = bank("proj", i)
                        if dst is None:
                            to = v_col[:, tiles(f), b * ROWS + 1:(b + 1) * ROWS:STEPS]
                            act.activation(to, ps[:, :].rearrange("p (n t) -> p n t", t=TB),
                                           ACT.Silu).then_inc(drained["proj"].handle, 1)
                        else:
                            act.activation(dst[:, f, tokens(b)], ps[:, :],
                                           ACT.Silu).then_inc(drained["proj"].handle, 1)
                        i += 1
                for w in range(3):
                    for b, f in halves:
                        filled["proj"].wait(act, g, i + 1)
                        ps = bank("proj", i)
                        src = ps[:, :]
                        if w == 0:
                            to = logf[:, f, b, :, 1:SLOTS]
                            src = src.rearrange("p (n t) -> p n t", t=TB)
                        else:
                            to = (beta_col if w == 1 else gate)[:, f, tokens(b)]
                        act.activation(to, src, ACT.Sigmoid).then_inc(drained["proj"].handle, 1)
                        i += 1
                out_stored.wait_previous(act, g)
                for i, (b, f) in enumerate(halves):
                    drained["proj"].wait(act, g, i + 1)
                    act.activation(ss_col[:, f, tokens(b)], k_col[:, f, tokens(b)],
                                   ACT.Square).then_inc(k_squared.handle, 1)
                for i, (b, f) in enumerate(halves):
                    f_floored.wait(act, g, i + 1)
                    act.activation(logf[:, f, b, :, 1:SLOTS], logf[:, f, b, :, 1:SLOTS],
                                   ACT.Ln).then_inc(f_logged.handle, 1)
                for i, (b, f) in enumerate(halves):
                    filled["kss"].wait(act, g, i + 1)
                    act.activation(ss_col[:, f, tokens(b)], bank("kss", i)[:, :], ACT.Ln,
                                   bias=eps2).then_inc(drained["kss"].handle, 1)
                for i, (b, f) in enumerate(halves):
                    drained["kss"].wait(act, g, i + 1)
                    act.activation(ss_col[:, f, tokens(b)], ss_col[:, f, tokens(b)], ACT.Exp,
                                   scale=-0.5).then_inc(r_ready.handle, 1)
                for f in range(HF):
                    centred.wait(act, g, GB * (f + 1))
                    act.activation(ep[:, f, :, :, :], dd4[:, f, :, :, :], ACT.Exp).then_inc(ep_ready.handle, 1)
                    act.activation(em[:, f, :, :, :], dd4[:, f, :, :, :], ACT.Exp,
                                   scale=-1.0).then_inc(em_ready.handle, 1)
                low5 = low.rearrange("p (i h b j) -> p i h b j", h=HPH, b=GB, i=ROWS)
                u_ready.wait(act, g, GB * HF * STEPS)
                for i in range(8):
                    b, r = i // 4, 4 * (i % 4)
                    filled["nt"].wait(act, g, i + 1)
                    src = bank("nt", i)[:, :].rearrange("p (i h b j) -> p i h b j", i=4, h=HPH, b=GB)[:, :, :, b, :]
                    act.activation(low5[:, r:r + 4, :, b, :], src,
                                   ACT.Copy).then_inc(drained["nt"].handle, 1)
                rows_turned.wait(act, g, 3 * HF)
                filled["a"].wait(act, g, TILES // 8)
                for i in range(4):
                    filled["tt"].wait(act, g, i + 1)
                    src = bank("tt", i)[:, :].rearrange("p (i m) -> p i m", i=4)
                    for b in range(GB):
                        r = b * ROWS + 4 * i
                        last = act.activation(t_t[:, :, r:r + 4].rearrange("p m i -> p i m"), src, ACT.Copy,
                                              scale=cf[:, C_BATCH + b:C_BATCH + b + 1])
                    last.then_inc(drained["tt"].handle, 1)
                for i in range(TILES // 16):
                    filled["xu"].wait(act, g, i + 1)
                    act.activation(xu_t[:, 16 * i:16 * (i + 1), :],
                                   bank("xu", i)[:, :].rearrange("p (m i) -> p m i", i=HD),
                                   ACT.Copy, scale=-1.0).then_inc(drained["xu"].handle, 1)
                for k in range(NO):
                    o_filled.wait(act, g, k + 1)
                    src = psum[O_BANKS[k % 2]][:, :].rearrange("p (n f b t) -> p n f b t", f=HF, b=GB, t=TB)
                    for f in range(HF):
                        to = o_col[:, f, :].rearrange("p (b n t) -> p n b t", b=GB, t=TB)
                        act.activation(to[:, k * OSTEPS:(k + 1) * OSTEPS, :, :], src[:, :, f, :, :],
                                       ACT.Copy).then_inc(o_copied.handle, 1)
                for i, (b, f) in enumerate(halves):
                    y_ready.wait(act, g, i + 1)
                    act.activation(r_col[:, f, tokens(b)], y_col[:, f, tokens(b)],
                                   ACT.Square).then_inc(y_squared.handle, 1)
                for i, (b, f) in enumerate(halves):
                    filled["yss"].wait(act, g, i + 1)
                    act.activation(r_col[:, f, tokens(b)], bank("yss", i)[:, :], ACT.Ln, scale=1.0 / HD,
                                   bias=eps2).then_inc(drained["yss"].handle, 1)
                    drained["yss"].wait(act, g, i + 1)
                    act.activation(r_col[:, f, tokens(b)], r_col[:, f, tokens(b)], ACT.Exp,
                                   scale=-0.5).then_inc(yr_ready.handle, 1)
                for ln in range(2):
                    mean_ready.wait(act, g, (ln + 1) * TT)
                    act.activation(rstd[:, :], mean_var[:, :, 1], ACT.Ln, bias=eps_ln).then_inc(var_logged.handle, 1)
                    var_logged.wait(act, g, ln + 1)
                    act.activation(rstd[:, :], rstd[:, :], ACT.Exp, scale=-0.5).then_inc(rstd_ready.handle, 1)
                    if ln == 0:
                        for i in range(TT // 2):
                            filled["ht"].wait(act, g, i + 1)
                            act.activation(h_col[:, :, 2 * i * P:2 * (i + 1) * P],
                                           bank("ht", i)[:, :].rearrange("p (a t) -> p a t", a=KT),
                                           ACT.Copy).then_inc(drained["ht"].handle, 1)

        @block.vector
        def _(dve):
            dve.wait_ge(weights_in.handle, n_weights)
            dve.wait_ge(lora_step.handle, 1)
            dve.tensor_copy(lora_a[:, :], psum[0][0:RANK, 0:D]).then_inc(lora_copied.handle, 1)
            dve.wait_ge(lora_step.handle, 2)
            dve.tensor_copy(lora_b[:, :], psum[1][0:UD, 0:D]).then_inc(lora_copied.handle, 1)
            dve.wait_ge(lora_step.handle, 2 + KT)
            for a in range(KT):
                dve.tensor_tensor(w_ffn[:, a, :], w_ffn[:, a, :], psum[2][:, a * D:(a + 1) * D],
                                  ALU.add).then_inc(lora_copied.handle, 1)
            dve.wait_ge(set_up.handle, 4)
            carry = v_row[:, :, :].rearrange("p m c -> p (m c)")
            with dve.Fori(0, G) as g:
                for b in range(GB):
                    filled["small"].wait(dve, g, b + 1)
                    dve.tensor_copy(small[0:SMALL, tokens(b)],
                                    bank("small", b)[0:SMALL, :]).then_inc(drained["small"].handle, 1)
                carry4 = carry[:, 0:GB * NBLK * SLOTS].rearrange("p (n s) -> p n s", s=SLOTS)
                dve.memset(carry4, 1.0).then_inc(carry_set.handle, 1)
                wait_apart(dve, g, (carry_set, 1))
                dve.memset(carry4[:, :, 0:1], 0.0).then_inc(carry_set.handle, 1)
                carry_set.wait(dve, g, 2)
                for i, (b, f) in enumerate(halves):
                    drained["proj"].wait(dve, g, 3 * GB * HF + i + 1)
                    dve.tensor_scalar(logf[:, f, b, :, 1:SLOTS], logf[:, f, b, :, 1:SLOTS], MIN_DECAY, None,
                                      ALU.max).then_inc(f_floored.handle, 1)
                for f in range(HF):
                    f_logged.wait(dve, g, GB * HF)
                    dve.tensor_tensor_scan(ep[:, f, :, :, :].rearrange("p b n s -> p (b n s)"),
                                           carry[:, 0:GB * NBLK * SLOTS],
                                           logf[:, f, :, :, :].rearrange("p b n s -> p (b n s)"),
                                           0.0, ALU.mult, ALU.add).then_inc(summed.handle, 1)
                for f in range(HF):
                    summed.wait(dve, g, f + 1)
                    filled["proj"].wait(dve, g, 6 * GB * HF)
                    for b in range(GB):
                        mid = ep[:, f, b, :, TB // 2:TB // 2 + 1].to_broadcast([P, NBLK, SLOTS])
                        dve.tensor_tensor(dd4[:, f, b, :, :], ep[:, f, b, :, :], mid,
                                          ALU.subtract).then_inc(centred.handle, 1)
                for i, (b, f) in enumerate(halves):
                    r_ready.wait(dve, g, i + 1)
                    dve.tensor_tensor(k_col[:, f, tokens(b)], k_col[:, f, tokens(b)], ss_col[:, f, tokens(b)],
                                      ALU.mult).then_inc(k_normed.handle, 1)
                for i, (b, f) in enumerate(halves):
                    k_normed.wait(dve, g, i + 1)
                    drained["proj"].wait(dve, g, 4 * GB * HF + i + 1)
                    dve.scalar_tensor_tensor(beta_col[:, f, tokens(b)], beta_col[:, f, tokens(b)], 2.0,
                                             k_col[:, f, tokens(b)], ALU.mult, ALU.mult).then_inc(kb_ready.handle, 1)
                for i, (b, f) in enumerate(halves):
                    kb_ready.wait(dve, g, i + 1)
                    ep_ready.wait(dve, g, f + 1)
                    for s in range(STEPS):
                        dve.tensor_tensor(uq[:, tiles(f), b * ROWS + s:(b + 1) * ROWS:STEPS], blocks(beta_col, b, f),
                                          ep[:, f, b, :, s:s + TB], ALU.mult).then_inc(u_ready.handle, 1)
                drained["proj"].wait(dve, g, 3 * GB * HF)
                u_ready.wait(dve, g, GB * HF * STEPS)
                w_ready.wait(dve, g, GB * HF * STEPS)
                q_ready.wait(dve, g, GB * HF)
                for f in range(HF):
                    dve.transpose(v_row[:, tiles(f), :], v_col[:, tiles(f), :]).then_inc(rows_turned.handle, 1)
                    dve.transpose(u_row[:, tiles(f), :], uq[:, tiles(f), 0:HD]).then_inc(rows_turned.handle, 1)
                    dve.transpose(w_row[:, tiles(f), :], w_col[:, tiles(f), :]).then_inc(rows_turned.handle, 1)
                for i in range(TILES // 8):
                    wait_apart(dve, g, (filled["a"], i + 1), (a_cleared, 1))
                    ps = bank("a", i)[:, 0:8 * 48].rearrange("p (m i) -> p m i", i=48)
                    dve.copy_predicated(a_t[:, 8 * i:8 * (i + 1), :],
                                        ci[:, M_LOW:M_LOW + HD].unsqueeze(1).to_broadcast([P, 8, HD]), ps[:, :, 0:HD])
                    dve.copy_predicated(aq[:, 8 * i:8 * (i + 1), :],
                                        ci[:, M_Q:M_END].unsqueeze(1).to_broadcast([P, 8, GB * TB]),
                                        ps[:, :, HD:48]).then_inc(drained["a"].handle, 1)
                inv4 = inv.rearrange("p (i k j) -> p i k j", i=ROWS, j=ROWS)
                low4 = low.rearrange("p (i k j) -> p i k j", i=ROWS, j=ROWS)
                eye = cf[:, C_EYE:C_EYE + ROWS * ROWS].rearrange("p (i j) -> p i j", i=ROWS)
                dve.tensor_copy(inv4, eye.unsqueeze(2).to_broadcast([P, ROWS, GB * HPH, ROWS])).then_inc(solve_step.handle, 1)
                drained["nt"].wait(dve, g, 8)
                for p in range(ROWS - 1):
                    below, width = ROWS - 1 - p, p + 1
                    size = [P, below, GB * HPH, width]
                    step = prod[:, 0:below * GB * HPH * width].rearrange("p (r k c) -> p r k c", r=below, c=width)
                    solve_step.wait(dve, g, 2 * p + 1)
                    dve.tensor_tensor(step, low4[:, p + 1:ROWS, :, p:p + 1].to_broadcast(size),
                                      inv4[:, p:p + 1, :, 0:width].to_broadcast(size),
                                      ALU.mult).then_inc(solve_step.handle, 1)
                    solve_step.wait(dve, g, 2 * p + 2)
                    dve.tensor_tensor(inv4[:, p + 1:ROWS, :, 0:width], inv4[:, p + 1:ROWS, :, 0:width], step,
                                      ALU.subtract).then_inc(solve_step.handle, 1)
                dve.memset(state[:, :, :, :], 0.0).then_inc(state_ready.handle, 1)
                edge_ready.wait(dve, g, GB * HF)
                mask = cf[:, C_HALF:C_HALF + GB * HD].unsqueeze(1).to_broadcast([P, HF, GB * HD])
                for n in range(NBLK):
                    us_filled.wait(dve, g, n + 1)
                    us = psum[US_BANKS[n % 2]][:, 0:HF * GB * HD].rearrange("p (f v) -> p f v", f=HF)
                    dve.tensor_tensor(delta[:, :, :, :].rearrange("p f b v -> p f (b v)"), us, mask,
                                      ALU.mult).then_inc(delta_ready.handle, 1)
                    if n == NBLK - 1:
                        break
                    s_filled.wait(dve, g, n + 1)
                    dve.tensor_tensor(moved[:, :, :, :].rearrange("p f b v -> p (f b v)"),
                                      state[:, :, :, :].rearrange("p f b v -> p (f b v)"),
                                      psum[S_BANK][:, 0:HF * GB * HD], ALU.add).then_inc(moved_ready.handle, 1)
                    moved_ready.wait(dve, g, n + 1)
                    dve.tensor_tensor(state[:, :, :, :], moved[:, :, :, :],
                                      edge[:, :, n, :].unsqueeze(3).to_broadcast([P, HF, GB, HD]),
                                      ALU.mult).then_inc(state_ready.handle, 1)
                o_copied.wait(dve, g, NO * HF)
                for i, (b, f) in enumerate(halves):
                    dve.tensor_tensor(y_col[:, f, tokens(b)], o_col[:, f, tokens(b)], gate[:, f, tokens(b)],
                                      ALU.mult).then_inc(y_ready.handle, 1)
                for i, (b, f) in enumerate(halves):
                    yr_ready.wait(dve, g, i + 1)
                    dve.scalar_tensor_tensor(y_col[:, f, tokens(b)], y_col[:, f, tokens(b)], norm_col[:, f:f + 1],
                                             r_col[:, f, tokens(b)], ALU.mult, ALU.mult).then_inc(y_normed.handle, 1)
                x_row_in.wait(dve, g, 16)
                for ln in range(2):
                    stage = "wo" if ln == 0 else "ff"
                    for i in range(TT // 2):
                        if ln == 1:
                            bias_added.wait(dve, g, 2 * i + 2)
                        filled[stage].wait(dve, g, i + 1)
                        dve.tensor_tensor(h_row[:, 2 * i:2 * i + 2, :], h_row[:, 2 * i:2 * i + 2, :],
                                          bank(stage, i)[:, :].rearrange("p (t c) -> p t c", c=D),
                                          ALU.add).then_inc(drained[stage].handle, 1)
                    for t in range(TT):
                        drained[stage].wait(dve, g, t // 2 + 1)
                        dve.bn_stats(stats[:, t, :], h_row[:, t, :]).then_inc(stats_ready.handle, 1)
                    for t in range(TT):
                        wait_apart(dve, g, (stats_ready, ln * TT + t + 1))
                        dve.bn_aggr(mean_var[:, t, :], stats[:, t, :]).then_inc(mean_ready.handle, 1)
                    rstd_ready.wait(dve, g, ln + 1)
                    for t in range(TT):
                        dve.tensor_scalar(h_row[:, t, :], h_row[:, t, :], mean_var[:, t, 0:1], rstd[:, t:t + 1],
                                          ALU.subtract, ALU.mult).then_inc(h_normed.handle, 1)


_ARGS = ["x", "xt", "Wq", "Wk", "Wv", "Wf1", "Wf2", "Wbeta", "Wog1", "Wog2", "norm_w", "Wo", "ffn_wt", "ffn_b",
         "lora_down_t", "lora_up_t", "down_aux", "up_aux_t", "const_f", "const_i"]


def kernel(**inputs):
    import concourse.bacc as _bacc
    from concourse import mybir as _mybir
    from concourse.bass_utils import run_bass_kernel_spmd as _run

    a = {k: np.asarray(v) for k, v in inputs.items()}
    x = a["L0_attn_x"]
    laid = {"x": x, "xt": x.reshape(-1, x.shape[-1]).T,
            "ffn_wt": a["L0_ffn_W"].T, "ffn_b": a["L0_ffn_b"],
            "lora_down_t": a["L0_ffn_lora_down"].T, "lora_up_t": a["L0_ffn_lora_up"].T,
            "down_aux": a["L0_ffn_down_aux"], "up_aux_t": a["L0_ffn_up_aux"].T}
    for name in ("Wq", "Wk", "Wv", "Wf1", "Wf2", "Wbeta", "Wog1", "Wog2", "Wo"):
        laid[name] = a["L0_attn_" + name]
    laid["norm_w"] = a["L0_attn_norm_w"].reshape(HF, P).T
    laid["const_f"], laid["const_i"] = constants()

    nc = _bacc.Bacc("TRN2", target_bir_lowering=False, num_devices=1)
    arrays, args = {}, []
    for name in _ARGS:
        v = np.ascontiguousarray(laid[name])
        arrays[f"in_{name}_dram"] = v
        args.append(nc.dram_tensor(f"in_{name}_dram", v.shape, _mybir.dt.from_np(v.dtype), kind="ExternalInput").ap())
    args.append(nc.dram_tensor("out_0_dram", x.shape, _mybir.dt.from_np(x.dtype), kind="ExternalOutput").ap())
    delta_block(nc, *args)
    r = _run(nc, [arrays], core_ids=[0])
    return r.results[0]["out_0_dram"]
```

```python
from contextlib import ExitStack

import numpy as np

import concourse.bass as bass
from concourse import mybir

ALU = mybir.AluOpType
ACT = mybir.ActivationFunctionType
F32 = mybir.dt.float32
I32 = mybir.dt.int32

P = 128
H, HD = 8, 32
D = H * HD
HF = D // P
HPH = P // HD
GB = 2
PAIRS = 4
SEG = 128
TB = 8
STEPS = 2
ROWS = TB * STEPS
RQ = ROWS + TB
BANK = 512
L2_EPS = 1e-6
RMS_EPS = 1e-6
LN_EPS = 1e-5
MIN_DECAY = 2.0 ** -24

C_IDENT = 0
C_HEADS = C_IDENT + P
C_EXPAND = C_HEADS + P
C_BATCH = C_EXPAND + D
C_HALF = C_BATCH + GB
C_EYE = C_HALF + GB * HD
C_EPS = C_EYE + ROWS * ROWS
C_END = C_EPS + 2
M_LOW = 0
M_Q = M_LOW + GB * ROWS
M_END = M_Q + GB * TB


def constants():
    f = np.zeros((P, C_END), np.float32)
    p = np.arange(P)
    f[:, C_IDENT:C_IDENT + P] = np.eye(P)
    f[:, C_HEADS:C_HEADS + P] = p[:, None] // HD == p[None] // HD
    for h in range(H):
        f[2 * HD + h, C_EXPAND + h * HD:C_EXPAND + (h + 1) * HD] = 1
    batch = p % HD // ROWS
    for b in range(GB):
        f[:, C_BATCH + b] = batch == b
        f[:, C_HALF + b * HD:C_HALF + (b + 1) * HD] = (batch == b)[:, None]
    f[:, C_EYE:C_EYE + ROWS * ROWS] = np.eye(ROWS).ravel()
    f[:, C_EPS] = L2_EPS
    f[:, C_EPS + 1] = LN_EPS
    m = np.zeros((P, M_END), np.int32)
    row = p % ROWS
    for b in range(GB):
        m[:, M_LOW + b * ROWS:M_LOW + (b + 1) * ROWS] = (batch == b)[:, None] & (row[:, None] < np.arange(ROWS))
        m[:, M_Q + b * TB:M_Q + (b + 1) * TB] = (batch == b)[:, None] & (row[:, None] // STEPS <= np.arange(TB))
    return f, m


class Signal:

    def __init__(self, handle, each, primed=False):
        self.handle, self.each, self.primed = handle, each, primed
        self.base = each if primed else 0

    def wait(self, engine, g, count):
        assert 0 < count <= self.each
        engine.wait_ge(self.handle, g * self.each + (self.base + count))

    def wait_previous(self, engine, g):
        assert self.primed
        engine.wait_ge(self.handle, g * self.each + self.base)


def delta_block(nc, x, xt, wq, wk, wv, wf1, wf2, wbeta, wog1, wog2, norm_w, wo, ffn_wt, ffn_b,
                lora_down_t, lora_up_t, down_aux, up_aux_t, const_f, const_i, const_keep, out):
    G, TOK, _ = x.shape
    NT = PAIRS * SEG
    NBLK = NT // TB
    LEN = SEG // TB
    TILES = HF * NBLK
    assert TILES == P and NT == BANK and GB * ROWS == HD
    TT = TOK // P
    KT = D // P
    SLOTS = TB + 1
    SMALL = 2 * HD + H
    RANK, DD = lora_down_t.shape[1], lora_down_t.shape[0]
    UD = up_aux_t.shape[0]

    STAGES = [("small", GB), ("proj", 6 * GB * HF), ("kss", GB * HF), ("a", TILES // 8), ("nt", 8), ("tt", 4),
              ("xu", TILES // 16), ("xv", TILES // 16), ("yss", GB * HF), ("wo", TT // 2), ("ht", TT // 2), ("ff", TT // 2)]
    RING = 4
    FILLS = [(s, i) for s, n in STAGES for i in range(n)]
    AT = {f: n for n, f in enumerate(FILLS)}
    USO_BANKS, S_BANKS = (4, 5), (6, 7)
    TEAMS = 2
    TP = PAIRS // TEAMS
    TURNS = LEN * TEAMS

    with ExitStack() as ctx:
        def sb(name, shape, dt=F32):
            return ctx.enter_context(nc.sbuf_tensor(name, shape, dt))

        def signal(name, each, primed=False):
            made = Signal(ctx.enter_context(nc.semaphore(name)), each, primed)
            if primed:
                primed_signals.append(made)
            return made

        primed_signals = []

        w_kqv = sb("w_kqv", [P, KT, 3, D])
        w_small = sb("w_small", [P, KT, SMALL])
        w_second = sb("w_second", [P, D])
        w_out = sb("w_out", [P, HF, D])
        w_ffn = sb("w_ffn", [P, KT, D])
        bias_row = sb("bias_row", [P, D])
        norm_col = sb("norm_col", [P, HF])
        cf = sb("cf", [P, C_END])
        keep = sb("keep", [P, 1])
        ci = sb("ci", [P, M_END], I32)
        x_col = sb("x_col", [P, KT, TOK])
        scratch = sb("scratch", [P, 4, HF * TOK])
        logf = sb("logf", [P, HF, GB, NBLK, SLOTS])
        dd = sb("dd", [P, HF * GB * NBLK * SLOTS])
        epm = sb("epm", [P, 2, HF * GB * NBLK * SLOTS])
        uq = sb("uq", [P, TILES, GB, RQ])
        w_col = sb("w_col", [P, TILES, HD])
        v_col = sb("v_col", [P, TILES, HD])
        gate = sb("gate", [P, HF, TOK])
        edge = sb("edge", [P, LEN, PAIRS, HF, GB])
        enter = sb("enter", [P, PAIRS, HF, GB])
        w_row = sb("w_row", [P, TILES, HD])
        v_row = sb("v_row", [P, TILES, HD])
        aq = sb("aq", [P, TILES, GB * TB])
        prod = sb("prod", [P, GB * HPH * ROWS * ROWS // 4])
        state = sb("state", [P, PAIRS, HF, GB, HD])
        moved = sb("moved", [P, PAIRS, HF, GB, HD])
        delta_t = sb("delta_t", [P, PAIRS, HF, GB * ROWS])
        delta = sb("delta", [P, PAIRS, HF, HD])
        delta_own = sb("delta_own", [P, PAIRS, HF, GB, HD])
        stats = sb("stats", [P, TT, 6])
        mean_var = sb("mean_var", [P, TT, 2])
        rstd = sb("rstd", [P, TT])
        k_col, q_col, beta_col, ss_col = (scratch[:, i, :].rearrange("p (f t) -> p f t", f=HF) for i in range(4))
        u_row = scratch[:, 0:2, :].rearrange("p a (t c) -> p (a t) c", c=HD)
        low = scratch[:, 2, :]
        inv = scratch[:, 3, :]
        y_col, r_col = k_col, q_col
        h_col = beta_col
        h_row = scratch[:, 3, :].rearrange("p (t c) -> p t c", c=D)
        small = dd[:, 0:TOK]
        dd4 = dd[:, :].rearrange("p (f b n s) -> p f b n s", f=HF, b=GB, s=SLOTS)
        ep, em = (epm[:, i, :].rearrange("p (f b n s) -> p f b n s", f=HF, b=GB, s=SLOTS) for i in range(2))
        o_col = dd[:, 0:HF * TOK].rearrange("p (f t) -> p f t", f=HF)
        flat = epm[:, :, :].rearrange("p a b -> p (a b)")
        a_t = flat[:, 0:TILES * HD].rearrange("p (m i) -> p m i", i=HD)
        xv_t = a_t
        t_t = w_col
        lora_a = scratch[0:RANK, 3, 0:D]
        lora_b = scratch[0:UD, 3, D:2 * D]
        lora_d = x_col[0:DD, 0, 0:RANK]
        lora_u = x_col[0:RANK, 0, RANK:RANK + UD]
        aux_d = x_col[0:DD, 0, 256:256 + D]
        aux_u = x_col[0:UD, 0, 512:512 + D]

        ident = cf[:, C_IDENT:C_IDENT + P]
        same_head = cf[:, C_HEADS:C_HEADS + P]

        psum = [ctx.enter_context(nc.psum_tensor(f"bank{i}", [P, BANK], F32)) for i in range(8)]

        def bank(stage, i):
            return psum[AT[(stage, i)] % RING]

        weights_in = signal("weights_in", 0)
        lora_step = signal("lora_step", 0)
        lora_copied = signal("lora_copied", 0)
        set_up = signal("set_up", 0)
        x_col_in = signal("x_col_in", 16)
        keep_in = signal("keep_in", 16)
        x_row_in = signal("x_row_in", 16)
        out_stored = signal("out_stored", 16, primed=True)
        filled = {s: signal(f"{s}_filled", n, primed=s in ("proj", "ff")) for s, n in STAGES}
        drained = {s: signal(f"{s}_drained", n, primed=s == STAGES[-1][0]) for s, n in STAGES}
        k_squared = signal("k_squared", GB * HF)
        f_floored = signal("f_floored", GB * HF)
        f_logged = signal("f_logged", GB * HF)
        r_ready = signal("r_ready", GB * HF)
        k_normed = signal("k_normed", GB * HF)
        kb_ready = signal("kb_ready", GB * HF)
        carry_set = signal("carry_set", 2)
        summed = signal("summed", HF)
        centred = signal("centred", GB * HF)
        ep_ready = signal("ep_ready", HF)
        em_ready = signal("em_ready", HF)
        u_ready = signal("u_ready", GB * HF * STEPS)
        w_ready = signal("w_ready", GB * HF * STEPS)
        q_ready = signal("q_ready", GB * HF)
        edge_ready = signal("edge_ready", 3 * GB * HF, primed=True)
        rows_turned = signal("rows_turned", 3 * HF)
        a_cleared = signal("a_cleared", 1)
        solve_step = signal("solve_step", 1 + 2 * (ROWS - 1))
        uso_filled = signal("uso_filled", TURNS)
        delta_t_ready = signal("delta_t_ready", TURNS)
        delta_ready = signal("delta_ready", TURNS)
        own_ready = signal("own_ready", TURNS)
        s_filled = signal("s_filled", TURNS)
        moved_ready = signal("moved_ready", TURNS)
        state_ready = signal("state_ready", TURNS + 1)
        o_filled = signal("o_filled", TURNS)
        o_copied = signal("o_copied", TURNS, primed=True)
        y_ready = signal("y_ready", GB * HF)
        y_squared = signal("y_squared", GB * HF)
        yr_ready = signal("yr_ready", GB * HF)
        y_normed = signal("y_normed", GB * HF)
        stats_ready = signal("stats_ready", 2 * TT)
        mean_ready = signal("mean_ready", 2 * TT)
        var_logged = signal("var_logged", 2)
        rstd_ready = signal("rstd_ready", 2)
        h_normed = signal("h_normed", 2 * TT)
        bias_added = signal("bias_added", TT)

        halves = [(b, f) for b in range(GB) for f in range(HF)]

        def tokens(b):
            return slice(b * NT, (b + 1) * NT)

        def blocks(col, b, f):
            return col[:, f, tokens(b)].rearrange("p (n t) -> p n t", t=TB)

        def tiles(f):
            return slice(f * NBLK, (f + 1) * NBLK)

        def quarter(h):
            return slice(h * HD, (h + 1) * HD)

        def tile(f, pair, n):
            return f * NBLK + pair * LEN + n

        def team(k):
            return range(k * TP, (k + 1) * TP)

        def uso_bank(k):
            return psum[USO_BANKS[k]][:, 0:TP * HF * GB * RQ].rearrange(
                "p (q f b r) -> p q f b r", q=TP, f=HF, b=GB)

        def s_bank(k):
            return psum[S_BANKS[k]][:, 0:TP * HF * GB * HD].rearrange("p (q f v) -> p q f v", q=TP, f=HF)

        n_weights = 0
        block = ctx.enter_context(nc.Block())

        wait_registers = {e.engine: [e.alloc_register(f"until{i}") for i in range(4)]
                          for e in (nc.tensor, nc.vector, nc.gpsimd)}

        def wait_apart(engine, g, *waits):
            values = []
            for (s, count), reg in zip(waits, wait_registers[engine.engine]):
                engine.reg_alu(reg, g, s.each, ALU.mult)
                engine.reg_add(reg, reg, s.base + count)
                values.append(engine.snap(reg))
            engine.wait_ge(set_up.handle, 5)
            for (s, _), v in zip(waits, values):
                engine.wait_ge(s.handle, v)

        loads = [(w_kqv[:, :, 0, :], wk.rearrange("(a p) n -> p a n", p=P)),
                 (w_kqv[:, :, 1, :], wq.rearrange("(a p) n -> p a n", p=P)),
                 (w_kqv[:, :, 2, :], wv.rearrange("(a p) n -> p a n", p=P)),
                 (w_small[:, :, 0:HD], wf1.rearrange("(a p) n -> p a n", p=P)),
                 (w_small[:, :, HD:2 * HD], wog1.rearrange("(a p) n -> p a n", p=P)),
                 (w_small[:, :, 2 * HD:SMALL], wbeta.rearrange("(a p) n -> p a n", p=P)),
                 (w_second[0:HD, :], wf2), (w_second[HD:2 * HD, :], wog2),
                 (w_second[2 * HD:SMALL, :], const_f[2 * HD:SMALL, C_EXPAND:C_EXPAND + D]),
                 (w_out[:, :, :], wo.rearrange("(a p) n -> p a n", p=P)),
                 (w_ffn[:, :, :], ffn_wt.rearrange("(a p) n -> p a n", p=P)),
                 (bias_row[:, :], ffn_b.rearrange("(a n) -> a n", a=1).to_broadcast([P, D])),
                 (norm_col[:, :], norm_w),
                 (cf[:, :], const_f), (ci[:, :], const_i),
                 (lora_d, lora_down_t), (lora_u, lora_up_t), (aux_d, down_aux), (aux_u, up_aux_t)]
        n_weights = 16 * len(loads)

        @block.sync
        def _(sp):
            for dst, src in loads:
                sp.dma_start(dst, src).then_inc(weights_in.handle, 16)
            sp.wait_ge(lora_step.handle, 4)
            xt_view = xt.rearrange("(a p) t -> p a t", p=P)
            rows = x.rearrange("g t d -> (g t) d").rearrange("(n p) d -> p n d", p=P)
            out_rows = out.rearrange("g t d -> (g t) d").rearrange("(n p) d -> p n d", p=P)
            keep_view = const_keep.rearrange("g p -> p g")
            with sp.Fori(0, G) as g:
                filled["proj"].wait_previous(sp, g)
                sp.dma_start(x_col[:, :, :], xt_view[:, :, bass.ds(g * TOK, TOK)]).then_inc(x_col_in.handle, 16)
                edge_ready.wait_previous(sp, g)
                sp.dma_start(keep[:, :], keep_view[:, bass.ds(g, 1)]).then_inc(keep_in.handle, 16)
                filled["tt"].wait(sp, g, 4)
                sp.dma_start(h_row, rows[:, bass.ds(g * TT, TT), :]).then_inc(x_row_in.handle, 16)
                h_normed.wait(sp, g, 2 * TT)
                sp.dma_start(out_rows[:, bass.ds(g * TT, TT), :], h_row).then_inc(out_stored.handle, 16)
            sp.wait_ge(out_stored.handle, out_stored.base + 16 * G)

        @block.gpsimd
        def _(pool):
            pool.memset(v_col[:, :, :], 0.0).then_inc(set_up.handle, 1)
            pool.memset(logf[:, :, :, :, :], 0.0).then_inc(set_up.handle, 1)
            pool.memset(aq[:, :, :], 0.0).then_inc(set_up.handle, 1)
            pool.memset(state[:, :, :, :, :], 0.0).then_inc(set_up.handle, 1)
            for s in primed_signals:
                pool.sem_inc(s.handle, s.each)
            pool.sem_inc(set_up.handle, 1)
            pool.wait_ge(weights_in.handle, n_weights)
            with pool.Fori(0, G) as g:
                for i, (b, f) in enumerate(halves):
                    drained["proj"].wait(pool, g, 2 * GB * HF)
                    ep_ready.wait(pool, g, f + 1)
                    pool.tensor_tensor(
                        uq[:, tiles(f), b, ROWS:RQ], blocks(q_col, b, f),
                        ep[:, f, b, :, 1:SLOTS], ALU.mult).then_inc(q_ready.handle, 1)
                keep_in.wait(pool, g, 16)
                for i, (b, f) in enumerate(halves):
                    k_normed.wait(pool, g, i + 1)
                    em_ready.wait(pool, g, f + 1)
                    for s in range(STEPS):
                        pool.tensor_tensor(
                            w_col[:, tiles(f), b * ROWS + s:(b + 1) * ROWS:STEPS], blocks(k_col, b, f),
                            em[:, f, b, :, s:s + TB], ALU.mult).then_inc(w_ready.handle, 1)
                    ends = ep[:, f, b, :, TB].rearrange("p (k n) -> p k n", n=LEN)
                    starts = em[:, f, b, :, 0].rearrange("p (k n) -> p k n", n=LEN)
                    to = edge[:, :, :, f, b].rearrange("p n k -> p k n")
                    pool.tensor_tensor(to[:, :, 0:LEN - 1], ends[:, :, 0:LEN - 1], starts[:, :, 1:LEN],
                                       ALU.mult).then_inc(edge_ready.handle, 1)
                    pool.tensor_copy(to[:, :, LEN - 1], ends[:, :, LEN - 1]).then_inc(edge_ready.handle, 1)
                    pool.tensor_scalar(enter[:, :, f, b], starts[:, :, 0], keep[:, 0:1], None,
                                       ALU.mult).then_inc(edge_ready.handle, 1)
                wait_apart(pool, g, (u_ready, GB * HF * STEPS), (w_ready, GB * HF * STEPS), (edge_ready, 3 * GB * HF))
                pool.memset(a_t, 0.0).then_inc(a_cleared.handle, 1)
                for t in range(TT):
                    if t % 2 == 0:
                        filled["ht"].wait(pool, g, t // 2 + 1)
                    pool.tensor_tensor(h_row[:, t, :], h_row[:, t, :], bias_row[:, :],
                                       ALU.add).then_inc(bias_added.handle, 1)

        @block.tensor
        def _(pe):
            pe.wait_ge(weights_in.handle, n_weights)
            pe.matmul(psum[0][0:RANK, 0:D], lora_d, aux_d, start=True, stop=True).then_inc(lora_step.handle, 1)
            pe.wait_ge(lora_copied.handle, 1)
            pe.matmul(psum[1][0:UD, 0:D], lora_u, lora_a, start=True, stop=True).then_inc(lora_step.handle, 1)
            pe.wait_ge(lora_copied.handle, 2)
            for a in range(KT):
                pe.matmul(psum[2][:, a * D:(a + 1) * D] if KT * D <= BANK else None, lora_b[:, a * P:(a + 1) * P],
                          aux_u, start=True, stop=True).then_inc(lora_step.handle, 1)
            pe.wait_ge(lora_copied.handle, 2 + KT)

            def last_read(stage, i):
                n = AT[(stage, i)]
                s, j = FILLS[n - RING]
                return drained[s], j + 1 if n >= RING else 0

            def claim(g, stage, i):
                s, count = last_read(stage, i)
                pe.wait_ge(s.handle, g * s.each + (s.base + count))
                assert s.base + count > 0
                return bank(stage, i)

            with pe.Fori(0, G) as g:
                x_col_in.wait(pe, g, 16)
                for b in range(GB):
                    ps = claim(g, "small", b)
                    for a in range(KT):
                        mm = pe.matmul(ps[0:SMALL, :], w_small[:, a, :], x_col[:, a, tokens(b)],
                                       start=a == 0, stop=a == KT - 1)
                    mm.then_inc(filled["small"].handle, 1)
                i = 0
                for w in range(3):
                    for b, f in halves:
                        ps = claim(g, "proj", i)
                        for a in range(KT):
                            mm = pe.matmul(ps[:, :], w_kqv[:, a, w, f * P:(f + 1) * P], x_col[:, a, tokens(b)],
                                           start=a == 0, stop=a == KT - 1)
                        mm.then_inc(filled["proj"].handle, 1)
                        i += 1
                drained["small"].wait(pe, g, GB)
                for lo, hi in ((0, HD), (2 * HD, SMALL), (HD, 2 * HD)):
                    for b, f in halves:
                        ps = claim(g, "proj", i)
                        pe.matmul(ps[:, :], w_second[lo:hi, f * P:(f + 1) * P], small[lo:hi, tokens(b)],
                                  start=True, stop=True).then_inc(filled["proj"].handle, 1)
                        i += 1
                for i, (b, f) in enumerate(halves):
                    ps = claim(g, "kss", i)
                    k_squared.wait(pe, g, i + 1)
                    pe.matmul(ps[:, :], same_head, ss_col[:, f, tokens(b)], start=True,
                              stop=True).then_inc(filled["kss"].handle, 1)
                for i in range(TILES // 8):
                    inputs = ((w_ready, GB * HF * STEPS), (u_ready, GB * HF * STEPS), (q_ready, GB * HF))
                    wait_apart(pe, g, last_read("a", i), *(inputs if i == 0 else ()))
                    ps = bank("a", i)
                    for j in range(8):
                        m = 8 * i + j
                        for h in range(HPH):
                            mm = pe.matmul(ps[quarter(h), j * 48:(j + 1) * 48], w_col[quarter(h), m, :],
                                           uq[quarter(h), m, :, :].rearrange("p b r -> p (b r)"), start=True, stop=True)
                    mm.then_inc(filled["a"].handle, 1)
                drained["a"].wait(pe, g, TILES // 8)
                for i in range(8):
                    ps = claim(g, "nt", i)
                    for j in range(4):
                        mm = pe.transpose(ps[:, j * P:(j + 1) * P], a_t[:, :, 4 * i + j], ident)
                    mm.then_inc(filled["nt"].handle, 1)
                solve_step.wait(pe, g, 1 + 2 * (ROWS - 1))
                for i in range(4):
                    ps = claim(g, "tt", i)
                    for j in range(4):
                        mm = pe.transpose(ps[:, j * P:(j + 1) * P], inv[:, (4 * i + j) * P:(4 * i + j + 1) * P], ident)
                    mm.then_inc(filled["tt"].handle, 1)
                for stage, rows in (("xu", u_row), ("xv", v_row)):
                    for i in range(TILES // 16):
                        inputs = ((drained["tt"], 4), (rows_turned, 3 * HF))
                        wait_apart(pe, g, last_read(stage, i), *(inputs if (stage, i) == ("xu", 0) else ()))
                        ps = bank(stage, i)
                        for j in range(16):
                            m = 16 * i + j
                            for h in range(HPH):
                                mm = pe.matmul(ps[quarter(h), j * HD:(j + 1) * HD], rows[quarter(h), m, :],
                                               t_t[quarter(h), m, :], start=True, stop=True)
                        mm.then_inc(filled[stage].handle, 1)

                for n in range(LEN):
                    for k in range(TEAMS):
                        waits = [(state_ready, (n - 1) * TEAMS + k + 2 if n > 0 else 1)]
                        if n == 0 and k == 0:
                            waits.append((drained["xu"], TILES // 16))
                        waits.append((o_copied, (n - 1) * TEAMS + k + 1 if n > 0 else 0))
                        wait_apart(pe, g, *waits)
                        for q in team(k):
                            for f in range(HF):
                                for b in range(GB):
                                    for h in range(HPH):
                                        mm = pe.matmul(uso_bank(k)[quarter(h), q - TP * k, f, b, :], state[quarter(h), q, f, b, :],
                                                       uq[quarter(h), tile(f, q, n), b, :],
                                                       start=q == TP * k and f == 0 and b == 0, stop=False,
                                                       skip_group_check=True)
                        mm.then_inc(uso_filled.handle, 1)
                    for k in range(TEAMS):
                        wait_apart(pe, g, (own_ready, n * TEAMS + k + 1))
                        for q in team(k):
                            for f in range(HF):
                                for h in range(HPH):
                                    mm = pe.matmul(s_bank(k)[quarter(h), q - TP * k, f, :],
                                                   w_row[quarter(h), tile(f, q, n), :],
                                                   delta_own[quarter(h), q, f, :, :], start=True, stop=True)
                        mm.then_inc(s_filled.handle, 1)
                        for q in team(k):
                            for f in range(HF):
                                for h in range(HPH):
                                    mm = pe.matmul(uso_bank(k)[quarter(h), q - TP * k, f, :, ROWS:RQ], delta[quarter(h), q, f, :],
                                                   aq[quarter(h), tile(f, q, n), :], start=False, stop=True,
                                                   skip_group_check=True)
                        mm.then_inc(o_filled.handle, 1)

                for i, (b, f) in enumerate(halves):
                    ps = claim(g, "yss", i)
                    y_squared.wait(pe, g, i + 1)
                    pe.matmul(ps[:, :], same_head, r_col[:, f, tokens(b)], start=True,
                              stop=True).then_inc(filled["yss"].handle, 1)
                for i in range(TT // 2):
                    ps = claim(g, "wo", i)
                    y_normed.wait(pe, g, HF * (2 * i * P // NT + 1))
                    for j in range(2):
                        t = 2 * i + j
                        for f in range(HF):
                            mm = pe.matmul(ps[:, j * D:(j + 1) * D], y_col[:, f, t * P:(t + 1) * P], w_out[:, f, :],
                                           start=f == 0, stop=f == HF - 1)
                    mm.then_inc(filled["wo"].handle, 1)
                for i in range(TT // 2):
                    ps = claim(g, "ht", i)
                    h_normed.wait(pe, g, 2 * i + 2)
                    for a in range(KT):
                        for j in range(2):
                            at = (a * 2 + j) * P
                            mm = pe.transpose(ps[:, at:at + P], h_row[:, 2 * i + j, a * P:(a + 1) * P], ident)
                    mm.then_inc(filled["ht"].handle, 1)
                for i in range(TT // 2):
                    ps = claim(g, "ff", i)
                    drained["ht"].wait(pe, g, i + 1)
                    for j in range(2):
                        t = 2 * i + j
                        for a in range(KT):
                            mm = pe.matmul(ps[:, j * D:(j + 1) * D], h_col[:, a, t * P:(t + 1) * P], w_ffn[:, a, :],
                                           start=a == 0, stop=a == KT - 1)
                    mm.then_inc(filled["ff"].handle, 1)

        @block.scalar
        def _(act):
            act.wait_ge(weights_in.handle, n_weights)
            act.wait_ge(set_up.handle, 5)
            eps2 = cf[:, C_EPS:C_EPS + 1]
            eps_ln = cf[:, C_EPS + 1:C_EPS + 2]
            with act.Fori(0, G) as g:
                filled["ff"].wait_previous(act, g)
                i = 0
                for w, dst in enumerate((k_col, q_col, None)):
                    for b, f in halves:
                        filled["proj"].wait(act, g, i + 1)
                        ps = bank("proj", i)
                        if dst is None:
                            to = v_col[:, tiles(f), b * ROWS + 1:(b + 1) * ROWS:STEPS]
                            act.activation(to, ps[:, :].rearrange("p (n t) -> p n t", t=TB),
                                           ACT.Silu).then_inc(drained["proj"].handle, 1)
                        else:
                            act.activation(dst[:, f, tokens(b)], ps[:, :],
                                           ACT.Silu).then_inc(drained["proj"].handle, 1)
                        i += 1
                for w in range(3):
                    for b, f in halves:
                        filled["proj"].wait(act, g, i + 1)
                        ps = bank("proj", i)
                        src = ps[:, :]
                        if w == 0:
                            to = logf[:, f, b, :, 1:SLOTS]
                            src = src.rearrange("p (n t) -> p n t", t=TB)
                        else:
                            to = (beta_col if w == 1 else gate)[:, f, tokens(b)]
                        act.activation(to, src, ACT.Sigmoid).then_inc(drained["proj"].handle, 1)
                        i += 1
                out_stored.wait_previous(act, g)
                for i, (b, f) in enumerate(halves):
                    drained["proj"].wait(act, g, i + 1)
                    act.activation(ss_col[:, f, tokens(b)], k_col[:, f, tokens(b)],
                                   ACT.Square).then_inc(k_squared.handle, 1)
                for i, (b, f) in enumerate(halves):
                    f_floored.wait(act, g, i + 1)
                    act.activation(logf[:, f, b, :, 1:SLOTS], logf[:, f, b, :, 1:SLOTS],
                                   ACT.Ln).then_inc(f_logged.handle, 1)
                for i, (b, f) in enumerate(halves):
                    filled["kss"].wait(act, g, i + 1)
                    act.activation(ss_col[:, f, tokens(b)], bank("kss", i)[:, :], ACT.Ln,
                                   bias=eps2).then_inc(drained["kss"].handle, 1)
                for i, (b, f) in enumerate(halves):
                    drained["kss"].wait(act, g, i + 1)
                    act.activation(ss_col[:, f, tokens(b)], ss_col[:, f, tokens(b)], ACT.Exp,
                                   scale=-0.5).then_inc(r_ready.handle, 1)
                for f in range(HF):
                    centred.wait(act, g, GB * (f + 1))
                    act.activation(ep[:, f, :, :, :], dd4[:, f, :, :, :], ACT.Exp).then_inc(ep_ready.handle, 1)
                    act.activation(em[:, f, :, :, :], dd4[:, f, :, :, :], ACT.Exp,
                                   scale=-1.0).then_inc(em_ready.handle, 1)
                low5 = low.rearrange("p (i h b j) -> p i h b j", h=HPH, b=GB, i=ROWS)
                u_ready.wait(act, g, GB * HF * STEPS)
                for i in range(8):
                    b, r = i // 4, 4 * (i % 4)
                    filled["nt"].wait(act, g, i + 1)
                    src = bank("nt", i)[:, :].rearrange("p (i h b j) -> p i h b j", i=4, h=HPH, b=GB)[:, :, :, b, :]
                    act.activation(low5[:, r:r + 4, :, b, :], src,
                                   ACT.Copy).then_inc(drained["nt"].handle, 1)
                rows_turned.wait(act, g, 3 * HF)
                filled["a"].wait(act, g, TILES // 8)
                for i in range(4):
                    filled["tt"].wait(act, g, i + 1)
                    src = bank("tt", i)[:, :].rearrange("p (i m) -> p i m", i=4)
                    for b in range(GB):
                        r = b * ROWS + 4 * i
                        last = act.activation(t_t[:, :, r:r + 4].rearrange("p m i -> p i m"), src, ACT.Copy,
                                              scale=cf[:, C_BATCH + b:C_BATCH + b + 1])
                    last.then_inc(drained["tt"].handle, 1)
                for i in range(TILES // 16):
                    filled["xu"].wait(act, g, i + 1)
                    act.activation(uq[:, 16 * i:16 * (i + 1), :, 0:ROWS],
                                   bank("xu", i)[:, :].rearrange("p (m b i) -> p m b i", b=GB, i=ROWS),
                                   ACT.Copy).then_inc(drained["xu"].handle, 1)
                for i in range(TILES // 16):
                    filled["xv"].wait(act, g, i + 1)
                    act.activation(xv_t[:, 16 * i:16 * (i + 1), :],
                                   bank("xv", i)[:, :].rearrange("p (m i) -> p m i", i=HD),
                                   ACT.Copy).then_inc(drained["xv"].handle, 1)
                to = o_col[:, :, :].rearrange("p f (b q n t) -> p n q f b t", b=GB, q=PAIRS, t=TB)
                for n in range(LEN):
                    for k in range(TEAMS):
                        o_filled.wait(act, g, n * TEAMS + k + 1)
                        for f in range(HF):
                            last = act.activation(to[:, n, k * TP:(k + 1) * TP, f, :, :],
                                                  uso_bank(k)[:, :, f, :, ROWS:RQ], ACT.Copy)
                        last.then_inc(o_copied.handle, 1)
                for i, (b, f) in enumerate(halves):
                    y_ready.wait(act, g, i + 1)
                    act.activation(r_col[:, f, tokens(b)], y_col[:, f, tokens(b)],
                                   ACT.Square).then_inc(y_squared.handle, 1)
                for i, (b, f) in enumerate(halves):
                    filled["yss"].wait(act, g, i + 1)
                    act.activation(r_col[:, f, tokens(b)], bank("yss", i)[:, :], ACT.Ln, scale=1.0 / HD,
                                   bias=eps2).then_inc(drained["yss"].handle, 1)
                    drained["yss"].wait(act, g, i + 1)
                    act.activation(r_col[:, f, tokens(b)], r_col[:, f, tokens(b)], ACT.Exp,
                                   scale=-0.5).then_inc(yr_ready.handle, 1)
                for ln in range(2):
                    mean_ready.wait(act, g, (ln + 1) * TT)
                    act.activation(rstd[:, :], mean_var[:, :, 1], ACT.Ln, bias=eps_ln).then_inc(var_logged.handle, 1)
                    var_logged.wait(act, g, ln + 1)
                    act.activation(rstd[:, :], rstd[:, :], ACT.Exp, scale=-0.5).then_inc(rstd_ready.handle, 1)
                    if ln == 0:
                        for i in range(TT // 2):
                            filled["ht"].wait(act, g, i + 1)
                            act.activation(h_col[:, :, 2 * i * P:2 * (i + 1) * P],
                                           bank("ht", i)[:, :].rearrange("p (a t) -> p a t", a=KT),
                                           ACT.Copy).then_inc(drained["ht"].handle, 1)

        @block.vector
        def _(dve):
            dve.wait_ge(weights_in.handle, n_weights)
            dve.wait_ge(lora_step.handle, 1)
            dve.tensor_copy(lora_a, psum[0][0:RANK, 0:D]).then_inc(lora_copied.handle, 1)
            dve.wait_ge(lora_step.handle, 2)
            dve.tensor_copy(lora_b, psum[1][0:UD, 0:D]).then_inc(lora_copied.handle, 1)
            dve.wait_ge(lora_step.handle, 2 + KT)
            for a in range(KT):
                dve.tensor_tensor(w_ffn[:, a, :], w_ffn[:, a, :], psum[2][:, a * D:(a + 1) * D],
                                  ALU.add).then_inc(lora_copied.handle, 1)
            dve.wait_ge(set_up.handle, 5)
            carry = v_row[:, :, :].rearrange("p m c -> p (m c)")
            with dve.Fori(0, G) as g:
                for b in range(GB):
                    filled["small"].wait(dve, g, b + 1)
                    dve.tensor_copy(small[0:SMALL, tokens(b)],
                                    bank("small", b)[0:SMALL, :]).then_inc(drained["small"].handle, 1)
                carry4 = carry[:, 0:GB * NBLK * SLOTS].rearrange("p (n s) -> p n s", s=SLOTS)
                dve.memset(carry4, 1.0).then_inc(carry_set.handle, 1)
                wait_apart(dve, g, (carry_set, 1))
                dve.memset(carry4[:, :, 0:1], 0.0).then_inc(carry_set.handle, 1)
                carry_set.wait(dve, g, 2)
                for i, (b, f) in enumerate(halves):
                    drained["proj"].wait(dve, g, 3 * GB * HF + i + 1)
                    dve.tensor_scalar(logf[:, f, b, :, 1:SLOTS], logf[:, f, b, :, 1:SLOTS], MIN_DECAY, None,
                                      ALU.max).then_inc(f_floored.handle, 1)
                for f in range(HF):
                    f_logged.wait(dve, g, GB * HF)
                    dve.tensor_tensor_scan(ep[:, f, :, :, :].rearrange("p b n s -> p (b n s)"),
                                           carry[:, 0:GB * NBLK * SLOTS],
                                           logf[:, f, :, :, :].rearrange("p b n s -> p (b n s)"),
                                           0.0, ALU.mult, ALU.add).then_inc(summed.handle, 1)
                for f in range(HF):
                    summed.wait(dve, g, f + 1)
                    filled["proj"].wait(dve, g, 6 * GB * HF)
                    for b in range(GB):
                        mid = ep[:, f, b, :, TB // 2:TB // 2 + 1].to_broadcast([P, NBLK, SLOTS])
                        dve.tensor_tensor(dd4[:, f, b, :, :], ep[:, f, b, :, :], mid,
                                          ALU.subtract).then_inc(centred.handle, 1)
                for i, (b, f) in enumerate(halves):
                    r_ready.wait(dve, g, i + 1)
                    dve.tensor_tensor(k_col[:, f, tokens(b)], k_col[:, f, tokens(b)], ss_col[:, f, tokens(b)],
                                      ALU.mult).then_inc(k_normed.handle, 1)
                for i, (b, f) in enumerate(halves):
                    k_normed.wait(dve, g, i + 1)
                    drained["proj"].wait(dve, g, 4 * GB * HF + i + 1)
                    dve.scalar_tensor_tensor(beta_col[:, f, tokens(b)], beta_col[:, f, tokens(b)], 2.0,
                                             k_col[:, f, tokens(b)], ALU.mult, ALU.mult).then_inc(kb_ready.handle, 1)
                for i, (b, f) in enumerate(halves):
                    kb_ready.wait(dve, g, i + 1)
                    ep_ready.wait(dve, g, f + 1)
                    for s in range(STEPS):
                        dve.tensor_tensor(uq[:, tiles(f), b, s:ROWS:STEPS], blocks(beta_col, b, f),
                                          ep[:, f, b, :, s:s + TB], ALU.mult).then_inc(u_ready.handle, 1)
                drained["proj"].wait(dve, g, 3 * GB * HF)
                u_ready.wait(dve, g, GB * HF * STEPS)
                w_ready.wait(dve, g, GB * HF * STEPS)
                q_ready.wait(dve, g, GB * HF)
                for f in range(HF):
                    dve.transpose(v_row[:, tiles(f), :], v_col[:, tiles(f), :]).then_inc(rows_turned.handle, 1)
                    dve.transpose(u_row[:, tiles(f), :], uq[:, tiles(f), :, 0:ROWS]).then_inc(rows_turned.handle, 1)
                    dve.transpose(w_row[:, tiles(f), :], w_col[:, tiles(f), :]).then_inc(rows_turned.handle, 1)
                for i in range(TILES // 8):
                    wait_apart(dve, g, (filled["a"], i + 1), (a_cleared, 1))
                    ps = bank("a", i)[:, 0:8 * GB * RQ].rearrange("p (m b r) -> p m b r", m=8, b=GB)
                    own = slice(8 * i, 8 * (i + 1))
                    for to, mask, src in ((a_t, ci[:, M_LOW:M_Q], ps[:, :, :, 0:ROWS]),
                                          (aq, ci[:, M_Q:M_END], ps[:, :, :, ROWS:RQ])):
                        last = dve.copy_predicated(
                            to[:, own, :].rearrange("p m (b r) -> p m b r", b=GB),
                            mask.rearrange("p (b r) -> p b r", b=GB).unsqueeze(1).to_broadcast(list(src.shape)), src)
                    last.then_inc(drained["a"].handle, 1)
                inv4 = inv.rearrange("p (i k j) -> p i k j", i=ROWS, j=ROWS)
                low4 = low.rearrange("p (i k j) -> p i k j", i=ROWS, j=ROWS)
                eye = cf[:, C_EYE:C_EYE + ROWS * ROWS].rearrange("p (i j) -> p i j", i=ROWS)
                dve.tensor_copy(inv4, eye.unsqueeze(2).to_broadcast([P, ROWS, GB * HPH, ROWS])).then_inc(solve_step.handle, 1)
                drained["nt"].wait(dve, g, 8)
                for p in range(ROWS - 1):
                    below, width = ROWS - 1 - p, p + 1
                    size = [P, below, GB * HPH, width]
                    step = prod[:, 0:below * GB * HPH * width].rearrange("p (r k c) -> p r k c", r=below, c=width)
                    solve_step.wait(dve, g, 2 * p + 1)
                    dve.tensor_tensor(step, low4[:, p + 1:ROWS, :, p:p + 1].to_broadcast(size),
                                      inv4[:, p:p + 1, :, 0:width].to_broadcast(size),
                                      ALU.mult).then_inc(solve_step.handle, 1)
                    solve_step.wait(dve, g, 2 * p + 2)
                    dve.tensor_tensor(inv4[:, p + 1:ROWS, :, 0:width], inv4[:, p + 1:ROWS, :, 0:width], step,
                                      ALU.subtract).then_inc(solve_step.handle, 1)
                edge_ready.wait(dve, g, 3 * GB * HF)
                flat_state = state[:, :, :, :, :].rearrange("p q f b v -> p (q f b) v")
                dve.tensor_tensor(flat_state, flat_state,
                                  enter[:, :, :, :].rearrange("p q f b -> p (q f b)").unsqueeze(2).to_broadcast(
                                      [P, PAIRS * HF * GB, HD]),
                                  ALU.mult).then_inc(state_ready.handle, 1)
                drained["xv"].wait(dve, g, TILES // 16)
                xv5 = xv_t.rearrange("p (f q n) r -> p n q f r", f=HF, q=PAIRS)
                own_batch = cf[:, C_HALF:C_HALF + GB * HD].rearrange("p (b v) -> p b v", b=GB)
                own_batch = own_batch.unsqueeze(1).to_broadcast([P, TP * HF, GB, HD])

                def tell_delta(n, k):
                    turn = n * TEAMS + k + 1
                    qs = slice(k * TP, (k + 1) * TP)
                    uso_filled.wait(dve, g, turn)
                    for f in range(HF):
                        last = dve.tensor_tensor(
                            delta_t[:, qs, f, :].rearrange("p q (b r) -> p q b r", b=GB),
                            xv5[:, n, qs, f, :].rearrange("p q (b r) -> p q b r", b=GB),
                            uso_bank(k)[:, :, f, :, 0:ROWS], ALU.subtract)
                    last.then_inc(delta_t_ready.handle, 1)
                    delta_t_ready.wait(dve, g, turn)
                    dve.transpose(delta[:, qs, :, :].rearrange("p q f v -> p (q f v)"),
                                  delta_t[:, qs, :, :].rearrange("p q f v -> p (q f v)")).then_inc(delta_ready.handle, 1)
                    delta_ready.wait(dve, g, turn)
                    dve.tensor_tensor(delta_own[:, qs, :, :, :].rearrange("p q f b v -> p (q f) b v"),
                                      delta[:, qs, :, :].rearrange("p q f v -> p (q f) v").unsqueeze(2).to_broadcast(
                                          [P, TP * HF, GB, HD]), own_batch, ALU.mult).then_inc(own_ready.handle, 1)

                for n in range(LEN):
                    for k in range(TEAMS):
                        tell_delta(n, k)
                    for k in range(TEAMS):
                        turn = n * TEAMS + k + 1
                        qs = slice(k * TP, (k + 1) * TP)
                        s_filled.wait(dve, g, turn)
                        dve.tensor_tensor(moved[:, qs, :, :, :].rearrange("p q f b v -> p (q f b v)"),
                                          state[:, qs, :, :, :].rearrange("p q f b v -> p (q f b v)"),
                                          s_bank(k)[:, :, :, :].rearrange("p q f v -> p (q f v)"),
                                          ALU.add).then_inc(moved_ready.handle, 1)
                        moved_ready.wait(dve, g, turn)
                        dve.tensor_tensor(
                            state[:, qs, :, :, :].rearrange("p q f b v -> p (q f b) v"),
                            moved[:, qs, :, :, :].rearrange("p q f b v -> p (q f b) v"),
                            edge[:, n, qs, :, :].rearrange("p q f b -> p (q f b)").unsqueeze(2).to_broadcast(
                                [P, TP * HF * GB, HD]), ALU.mult).then_inc(state_ready.handle, 1)
                o_copied.wait(dve, g, TURNS)
                for i, (b, f) in enumerate(halves):
                    dve.tensor_tensor(y_col[:, f, tokens(b)], o_col[:, f, tokens(b)], gate[:, f, tokens(b)],
                                      ALU.mult).then_inc(y_ready.handle, 1)
                for i, (b, f) in enumerate(halves):
                    yr_ready.wait(dve, g, i + 1)
                    dve.scalar_tensor_tensor(y_col[:, f, tokens(b)], y_col[:, f, tokens(b)], norm_col[:, f:f + 1],
                                             r_col[:, f, tokens(b)], ALU.mult, ALU.mult).then_inc(y_normed.handle, 1)
                x_row_in.wait(dve, g, 16)
                for ln in range(2):
                    stage = "wo" if ln == 0 else "ff"
                    for i in range(TT // 2):
                        if ln == 1:
                            bias_added.wait(dve, g, 2 * i + 2)
                        filled[stage].wait(dve, g, i + 1)
                        dve.tensor_tensor(h_row[:, 2 * i:2 * i + 2, :], h_row[:, 2 * i:2 * i + 2, :],
                                          bank(stage, i)[:, :].rearrange("p (t c) -> p t c", c=D),
                                          ALU.add).then_inc(drained[stage].handle, 1)
                    for t in range(TT):
                        drained[stage].wait(dve, g, t // 2 + 1)
                        dve.bn_stats(stats[:, t, :], h_row[:, t, :]).then_inc(stats_ready.handle, 1)
                    for t in range(TT):
                        wait_apart(dve, g, (stats_ready, ln * TT + t + 1))
                        dve.bn_aggr(mean_var[:, t, :], stats[:, t, :]).then_inc(mean_ready.handle, 1)
                    rstd_ready.wait(dve, g, ln + 1)
                    for t in range(TT):
                        dve.tensor_scalar(h_row[:, t, :], h_row[:, t, :], mean_var[:, t, 0:1], rstd[:, t:t + 1],
                                          ALU.subtract, ALU.mult).then_inc(h_normed.handle, 1)


_ARGS = ["x", "xt", "Wq", "Wk", "Wv", "Wf1", "Wf2", "Wbeta", "Wog1", "Wog2", "norm_w", "Wo", "ffn_wt", "ffn_b",
         "lora_down_t", "lora_up_t", "down_aux", "up_aux_t", "const_f", "const_i",
         "const_keep"]


def kernel(**inputs):
    import concourse.bacc as _bacc
    from concourse import mybir as _mybir
    from concourse.bass_utils import run_bass_kernel_spmd as _run

    a = {k: np.asarray(v) for k, v in inputs.items()}
    x = a["L0_attn_x"]
    batches, length, width = x.shape
    segments = length // SEG
    grid = (batches // (GB * PAIRS), GB * PAIRS, segments, SEG, width)
    grouped = x.reshape(grid).transpose(0, 2, 1, 3, 4).reshape(-1, GB * PAIRS * SEG, width)
    laid = {"x": grouped, "xt": grouped.reshape(-1, width).T,
            "ffn_wt": a["L0_ffn_W"].T, "ffn_b": a["L0_ffn_b"],
            "lora_down_t": a["L0_ffn_lora_down"].T, "lora_up_t": a["L0_ffn_lora_up"].T,
            "down_aux": a["L0_ffn_down_aux"], "up_aux_t": a["L0_ffn_up_aux"].T}
    for name in ("Wq", "Wk", "Wv", "Wf1", "Wf2", "Wbeta", "Wog1", "Wog2", "Wo"):
        laid[name] = a["L0_attn_" + name]
    laid["norm_w"] = a["L0_attn_norm_w"].reshape(HF, P).T
    laid["const_f"], laid["const_i"] = constants()
    laid["const_keep"] = np.broadcast_to((np.arange(len(grouped)) % segments != 0).astype(np.float32)[:, None],
                                         (len(grouped), P))

    nc = _bacc.Bacc("TRN2", target_bir_lowering=False, num_devices=1)
    arrays, args = {}, []
    for name in _ARGS:
        v = np.ascontiguousarray(laid[name])
        arrays[f"in_{name}_dram"] = v
        args.append(nc.dram_tensor(f"in_{name}_dram", v.shape, _mybir.dt.from_np(v.dtype), kind="ExternalInput").ap())
    args.append(nc.dram_tensor("out_0_dram", grouped.shape, _mybir.dt.from_np(x.dtype), kind="ExternalOutput").ap())
    delta_block(nc, *args)
    r = _run(nc, [arrays], core_ids=[0])
    o = np.asarray(r.results[0]["out_0_dram"]).reshape(grid[0], segments, GB * PAIRS, SEG, width)
    return o.transpose(0, 2, 1, 3, 4).reshape(x.shape)
```

```python
from contextlib import ExitStack

import numpy as np

import concourse.bass as bass
from concourse import mybir

ALU = mybir.AluOpType
ACT = mybir.ActivationFunctionType
F32 = mybir.dt.float32
I32 = mybir.dt.int32

P = 128
H, HD = 8, 32
D = H * HD
HF = D // P
HPH = P // HD
GB = 2
PAIRS = 4
SEG = 128
TB = 8
STEPS = 2
ROWS = TB * STEPS
RQ = ROWS + TB
BANK = 512
L2_EPS = 1e-6
RMS_EPS = 1e-6
LN_EPS = 1e-5
MIN_DECAY = 2.0 ** -24

C_IDENT = 0
C_HEADS = C_IDENT + P
C_EXPAND = C_HEADS + P
C_BATCH = C_EXPAND + D
C_EYE = C_BATCH + GB
C_EPS = C_EYE + ROWS * ROWS
C_END = C_EPS + 2
M_LOW = 0
M_Q = M_LOW + GB * ROWS
M_END = M_Q + GB * TB


def constants():
    f = np.zeros((P, C_END), np.float32)
    p = np.arange(P)
    f[:, C_IDENT:C_IDENT + P] = np.eye(P)
    f[:, C_HEADS:C_HEADS + P] = p[:, None] // HD == p[None] // HD
    for h in range(H):
        f[2 * HD + h, C_EXPAND + h * HD:C_EXPAND + (h + 1) * HD] = 1
    batch = p % HD // ROWS
    for b in range(GB):
        f[:, C_BATCH + b] = batch == b
    f[:, C_EYE:C_EYE + ROWS * ROWS] = np.eye(ROWS).ravel()
    f[:, C_EPS] = L2_EPS
    f[:, C_EPS + 1] = LN_EPS
    m = np.zeros((P, M_END), np.int32)
    row = p % ROWS
    for b in range(GB):
        m[:, M_LOW + b * ROWS:M_LOW + (b + 1) * ROWS] = (batch == b)[:, None] & (row[:, None] < np.arange(ROWS))
        m[:, M_Q + b * TB:M_Q + (b + 1) * TB] = (batch == b)[:, None] & (row[:, None] // STEPS <= np.arange(TB))
    return f, m


class After:

    def __init__(self, g):
        self.g = g


class Signal:

    def __init__(self, handle, each, primed=False):
        self.handle, self.each, self.primed = handle, each, primed
        self.base = each if primed else 0

    def offset(self, g, count):
        return self.base + count + (self.each if isinstance(g, After) else 0)

    def at(self, g, count):
        assert 0 < count <= self.each
        return (g.g if isinstance(g, After) else g) * self.each + self.offset(g, count)

    def before(self, g):
        assert self.primed
        return g * self.each + self.base


def delta_block(nc, x, xt, wq, wk, wv, wf1, wf2, wbeta, wog1, wog2, norm_w, wo, ffn_wt, ffn_b,
                lora_down_t, lora_up_t, down_aux, up_aux_t, const_f, const_i, const_keep, out):
    G, TOK, _ = x.shape
    NT = PAIRS * SEG
    NBLK = NT // TB
    LEN = SEG // TB
    TILES = HF * NBLK
    assert TILES == P and NT == BANK and GB * ROWS == HD
    TT = TOK // P
    KT = D // P
    SLOTS = TB + 1
    SMALL = 2 * HD + H
    RANK, DD = lora_down_t.shape[1], lora_down_t.shape[0]
    UD = up_aux_t.shape[0]

    STAGES = [("small", GB), ("f", GB * HF), ("kb", 2 * GB * HF), ("kss", GB * HF), ("q", GB * HF), ("a", TILES // 8),
              ("nt", 8), ("vg", 2 * GB * HF), ("tt", 4),
              ("xuv", TILES // 8), ("yss", GB * HF), ("wo", TT // 2), ("ht", TT // 2), ("ff", TT // 2)]
    RING = 6
    EARLY = ("small", "f")
    of = dict(STAGES)
    FILLS = [(s, i) for s in ("kb", "kss", "q", "a", "nt", "vg", "tt", "xuv", "small") for i in range(of[s])]
    FILLS += [(s, 2 * c + i) for c in range(2) for s in ("yss", "f") for i in range(2)]
    FILLS += [(s, i) for s in ("wo", "ht", "ff") for i in range(of[s])]
    assert len(FILLS) == sum(of.values()) and len(FILLS) % RING == 0
    AT = {f: n for n, f in enumerate(FILLS)}
    TEAM_BANKS = (6, 7)
    TEAMS = 2
    TP = PAIRS // TEAMS
    TURNS = LEN * TEAMS

    with ExitStack() as ctx:
        def sb(name, shape, dt=F32):
            return ctx.enter_context(nc.sbuf_tensor(name, shape, dt))

        def signal(name, each, primed=False):
            made = Signal(ctx.enter_context(nc.semaphore(name)), each, primed)
            if primed:
                primed_signals.append(made)
            return made

        primed_signals = []

        w_kqv = sb("w_kqv", [P, KT, 3, D])
        w_small = sb("w_small", [P, KT, SMALL])
        w_second = sb("w_second", [P, D])
        w_out = sb("w_out", [P, HF, D])
        w_ffn = sb("w_ffn", [P, KT, D])
        bias_row = sb("bias_row", [P, D])
        norm_col = sb("norm_col", [P, HF])
        cf = sb("cf", [P, C_END])
        keep = sb("keep", [P, 1])
        ci = sb("ci", [P, M_END], I32)
        x_col = sb("x_col", [P, KT, TOK])
        scratch = sb("scratch", [P, 6, HF * TOK])
        logf = sb("logf", [P, HF, GB, NBLK, SLOTS])
        dd = sb("dd", [P, HF * GB * NBLK * SLOTS])
        uq = sb("uq", [P, TILES, GB, RQ])
        w_col = sb("w_col", [P, TILES, HD])
        v_col = sb("v_col", [P, TILES, HD])
        gate = sb("gate", [P, HF, TOK])
        edge = sb("edge", [P, LEN, PAIRS, HF, GB])
        enter = sb("enter", [P, PAIRS, HF, GB])
        w_aq = sb("w_aq", [P, TILES, GB * HD + GB * TB])
        state = sb("state", [P, PAIRS, HF, GB, HD])
        qs = sb("qs", [P, PAIRS, HF, GB, TB])
        work = sb("work", [P, 3 * PAIRS * HF * GB * HD])
        stats = sb("stats", [P, TT, 6])
        mean_var = sb("mean_var", [P, TT, 2])
        rstd = sb("rstd", [P, TT])
        k_col, q_col, beta_col, ss_col = (scratch[:, i, :].rearrange("p (f t) -> p f t", f=HF) for i in range(4))
        uv_row = scratch[:, :, :].rearrange("p (w x) (t c) -> p w (x t) c", w=3, c=HD)[:, 0:3:2, :, :]
        u_row, v_row = uv_row[:, 0, :, :], uv_row[:, 1, :, :]
        low = scratch[:, 2, :]
        inv = scratch[:, 3, :]
        square_col = w_col[:, 0:TILES // 2, :].rearrange("p m c -> p (m c)").rearrange("p (f t) -> p f t", f=HF)
        y_col, r_col = k_col, q_col
        h_col = beta_col
        h_row = scratch[:, 3, :].rearrange("p (t c) -> p t c", c=D)
        small = scratch[:, 4, 0:TOK]
        dd4 = dd[:, :].rearrange("p (f b n s) -> p f b n s", f=HF, b=GB, s=SLOTS)
        ep, em, centre = (
            w_aq[:, :, i * GB * SLOTS:(i + 1) * GB * SLOTS].rearrange("p (f n) (b s) -> p f b n s", f=HF, b=GB)
            for i in range(3))
        w_row, aq = w_aq[:, :, 0:HD], w_aq[:, :, GB * HD:]
        a_t = w_aq[:, :, HD:GB * HD]
        moved = work[:, 0:PAIRS * HF * GB * HD]
        turned = work[:, PAIRS * HF * GB * HD:2 * PAIRS * HF * GB * HD]
        us_row, delta = (work[:, (4 + i) * PAIRS * HF * HD:(5 + i) * PAIRS * HF * HD] for i in range(2))
        delta4 = delta.rearrange("p (q f v) -> p q f v", q=PAIRS, f=HF)
        prod = work[:, 0:GB * HPH * ROWS * ROWS // 4]
        carry = work[:, 0:GB * NBLK * SLOTS]
        o_col = dd[:, 0:HF * TOK].rearrange("p (f t) -> p f t", f=HF)
        t_t = w_col
        lora_a = scratch[0:RANK, 3, 0:D]
        lora_b = scratch[0:UD, 3, D:2 * D]
        lora_d = x_col[0:DD, 0, 0:RANK]
        lora_u = x_col[0:RANK, 0, RANK:RANK + UD]
        aux_d = x_col[0:DD, 0, 256:256 + D]
        aux_u = x_col[0:UD, 0, 512:512 + D]

        ident = cf[:, C_IDENT:C_IDENT + P]
        same_head = cf[:, C_HEADS:C_HEADS + P]

        psum = [ctx.enter_context(nc.psum_tensor(f"bank{i}", [P, BANK], F32)) for i in range(8)]

        def bank(stage, i):
            return psum[AT[(stage, i)] % RING]

        weights_in = signal("weights_in", 0)
        lora_step = signal("lora_step", 0)
        lora_copied = signal("lora_copied", 0)
        set_up = signal("set_up", 0)
        x_col_in = signal("x_col_in", 16)
        keep_in = signal("keep_in", 16)
        x_row_in = signal("x_row_in", 16)
        out_stored = signal("out_stored", 16, primed=True)
        filled = {s: signal(f"{s}_filled", n, primed=s == "ff") for s, n in STAGES}
        drained = {s: signal(f"{s}_drained", n, primed=(s, n - 1) in FILLS[-RING:]) for s, n in STAGES}
        k_squared = signal("k_squared", GB * HF)
        f_floored = signal("f_floored", GB * HF)
        f_logged = signal("f_logged", GB * HF)
        r_ready = signal("r_ready", GB * HF)
        k_normed = signal("k_normed", GB * HF)
        kb_ready = signal("kb_ready", GB * HF)
        carry_set = signal("carry_set", 2)
        summed = signal("summed", HF)
        centred = signal("centred", GB * HF)
        ep_ready = signal("ep_ready", HF)
        em_ready = signal("em_ready", HF)
        u_ready = signal("u_ready", GB * HF * STEPS)
        w0_ready = signal("w0_ready", HF * STEPS)
        w1_ready = signal("w1_ready", HF * STEPS)
        xu_turned = signal("xu_turned", 2 * HF)
        w_parted = signal("w_parted", GB, primed=True)
        q_ready = signal("q_ready", GB * HF)
        edge_ready = signal("edge_ready", 3 * GB * HF)
        rows_turned = signal("rows_turned", 3 * HF)
        a_cleared = signal("a_cleared", 1)
        solve_step = signal("solve_step", 1 + 4 * (ROWS - 1))
        uso_filled = signal("uso_filled", TURNS)
        us_turned = signal("us_turned", TURNS)
        delta_ready = signal("delta_ready", TURNS)
        qs_copied = signal("qs_copied", TURNS)
        so_filled = signal("so_filled", TURNS)
        s_turned = signal("s_turned", TURNS)
        moved_ready = signal("moved_ready", TURNS)
        state_ready = signal("state_ready", TURNS + 1)
        o_ready = signal("o_ready", TURNS, primed=True)
        y_ready = signal("y_ready", GB * HF)
        y0_squared = signal("y0_squared", HF)
        y1_squared = signal("y1_squared", HF)
        yr_ready = signal("yr_ready", GB * HF)
        y_normed = signal("y_normed", GB * HF)
        stats_ready = signal("stats_ready", 2 * TT)
        mean_ready = signal("mean_ready", 2 * TT)
        std_ready = signal("std_ready", 4)
        rstd_ready = signal("rstd_ready", 4)
        h_normed = signal("h_normed", 2 * TT)
        bias_added = signal("bias_added", TT)

        halves = [(b, f) for f in range(HF) for b in range(GB)]

        by_batch = [(b, f) for b in range(GB) for f in range(HF)]

        def tokens(b):
            return slice(b * NT, (b + 1) * NT)

        def blocks(col, b, f):
            return col[:, f, tokens(b)].rearrange("p (n t) -> p n t", t=TB)

        def tiles(f):
            return slice(f * NBLK, (f + 1) * NBLK)

        def quarter(h):
            return slice(h * HD, (h + 1) * HD)

        def tile(f, pair, n):
            return f * NBLK + pair * LEN + n

        def team(k):
            return range(k * TP, (k + 1) * TP)

        def uso(k):
            return psum[TEAM_BANKS[k]][:, 0:TP * HF * GB * RQ].rearrange("p (q f b r) -> p q f b r", q=TP, f=HF, b=GB)

        def so(k):
            return psum[TEAM_BANKS[k]][:, TP * HF * GB * RQ:TP * HF * GB * (RQ + HD + TB)].rearrange(
                "p (q f r) -> p q f r", q=TP, f=HF)

        def w_half(engine, b, f, ready):
            for s in range(STEPS):
                engine.tensor_tensor(w_col[:, tiles(f), b * ROWS + s:(b + 1) * ROWS:STEPS], blocks(k_col, b, f),
                                     em[:, f, b, :, s:s + TB], ALU.mult).then_inc(ready.handle, 1)

        block = ctx.enter_context(nc.Block())

        wait_registers = {e.engine: [e.alloc_register(f"until{i}") for i in range(4)]
                          for e in (nc.tensor, nc.vector, nc.gpsimd)}

        def wait_apart(engine, g, *waits):
            at = g.g if isinstance(g, After) else g
            if isinstance(at, int):
                for s, count in waits:
                    engine.wait_ge(s.handle, at * s.each + s.offset(g, count))
                return
            values = []
            for (s, count), reg in zip(waits, wait_registers[engine.engine]):
                engine.reg_alu(reg, at, s.each, ALU.mult)
                engine.reg_add(reg, reg, s.offset(g, count))
                values.append(engine.snap(reg))
            engine.wait_ge(set_up.handle, 5)
            for (s, _), v in zip(waits, values):
                engine.wait_ge(s.handle, v)

        loads = [(w_kqv[:, :, 0, :], wk.rearrange("(a p) n -> p a n", p=P)),
                 (w_kqv[:, :, 1, :], wq.rearrange("(a p) n -> p a n", p=P)),
                 (w_kqv[:, :, 2, :], wv.rearrange("(a p) n -> p a n", p=P)),
                 (w_small[:, :, 0:HD], wf1.rearrange("(a p) n -> p a n", p=P)),
                 (w_small[:, :, HD:2 * HD], wog1.rearrange("(a p) n -> p a n", p=P)),
                 (w_small[:, :, 2 * HD:SMALL], wbeta.rearrange("(a p) n -> p a n", p=P)),
                 (w_second[0:HD, :], wf2), (w_second[HD:2 * HD, :], wog2),
                 (w_second[2 * HD:SMALL, :], const_f[2 * HD:SMALL, C_EXPAND:C_EXPAND + D]),
                 (w_out[:, :, :], wo.rearrange("(a p) n -> p a n", p=P)),
                 (w_ffn[:, :, :], ffn_wt.rearrange("(a p) n -> p a n", p=P)),
                 (bias_row[:, :], ffn_b.rearrange("(a n) -> a n", a=1).to_broadcast([P, D])),
                 (norm_col[:, :], norm_w),
                 (cf[:, :], const_f), (ci[:, :], const_i),
                 (lora_d, lora_down_t), (lora_u, lora_up_t), (aux_d, down_aux), (aux_u, up_aux_t)]
        n_weights = 16 * len(loads)

        @block.sync
        def _(sp):
            for dst, src in loads:
                sp.dma_start(dst, src).then_inc(weights_in.handle, 16)
            sp.wait_ge(lora_step.handle, 4)
            xt_view = xt.rearrange("(a p) t -> p a t", p=P)
            rows = x.rearrange("g t d -> (g t) d").rearrange("(n p) d -> p n d", p=P)
            out_rows = out.rearrange("g t d -> (g t) d").rearrange("(n p) d -> p n d", p=P)
            keep_view = const_keep.rearrange("g p -> p g")

            def load_columns(g):
                sp.dma_start(x_col[:, :, :], xt_view[:, :, bass.ds(g * TOK, TOK)]).then_inc(x_col_in.handle, 16)
                sp.dma_start(keep[:, :], keep_view[:, bass.ds(g, 1)]).then_inc(keep_in.handle, 16)

            def load_and_store(g, final):
                sp.wait_ge(filled["tt"].handle, filled["tt"].at(g, 4))
                sp.dma_start(h_row, rows[:, bass.ds(g * TT, TT), :]).then_inc(x_row_in.handle, 16)
                if not final:
                    sp.wait_ge(filled["vg"].handle, filled["vg"].at(g, 2 * GB * HF))
                    sp.wait_ge(edge_ready.handle, edge_ready.at(g, 3 * GB * HF))
                    load_columns(g + 1)
                sp.wait_ge(h_normed.handle, h_normed.at(g, 2 * TT))
                sp.dma_start(out_rows[:, bass.ds(g * TT, TT), :], h_row).then_inc(out_stored.handle, 16)

            load_columns(0)
            with sp.Fori(0, G - 1) as g:
                load_and_store(g, False)
            load_and_store(G - 1, True)
            sp.wait_ge(out_stored.handle, out_stored.base + 16 * G)

        @block.gpsimd
        def _(pool):
            pool.memset(v_col[:, :, :], 0.0).then_inc(set_up.handle, 1)
            pool.memset(logf[:, :, :, :, :], 0.0).then_inc(set_up.handle, 1)
            pool.memset(aq, 0.0).then_inc(set_up.handle, 1)
            pool.memset(state[:, :, :, :, :], 0.0).then_inc(set_up.handle, 1)
            for s in primed_signals:
                pool.sem_inc(s.handle, s.each)
            pool.sem_inc(set_up.handle, 1)
            pool.wait_ge(weights_in.handle, n_weights)
            def group(g, final):
                pool.wait_ge(keep_in.handle, keep_in.at(g, 16))
                for f in range(HF):
                    pool.wait_ge(k_normed.handle, k_normed.at(g, GB * (f + 1)))
                    pool.wait_ge(em_ready.handle, em_ready.at(g, f + 1))
                    w_half(pool, 1, f, w1_ready)
                    pool.wait_ge(ep_ready.handle, ep_ready.at(g, f + 1))
                    for b in range(GB):
                        pool.wait_ge(drained["q"].handle, drained["q"].at(g, GB * f + b + 1))
                        pool.tensor_tensor(uq[:, tiles(f), b, ROWS:RQ], blocks(q_col, b, f),
                                           ep[:, f, b, :, 1:SLOTS], ALU.mult).then_inc(q_ready.handle, 1)
                for b, f in halves:
                    ends = ep[:, f, b, :, TB].rearrange("p (k n) -> p k n", n=LEN)
                    starts = em[:, f, b, :, 0].rearrange("p (k n) -> p k n", n=LEN)
                    to = edge[:, :, :, f, b].rearrange("p n k -> p k n")
                    pool.tensor_tensor(to[:, :, 0:LEN - 1], ends[:, :, 0:LEN - 1], starts[:, :, 1:LEN],
                                       ALU.mult).then_inc(edge_ready.handle, 1)
                    pool.tensor_copy(to[:, :, LEN - 1], ends[:, :, LEN - 1]).then_inc(edge_ready.handle, 1)
                    pool.tensor_scalar(enter[:, :, f, b], starts[:, :, 0], keep[:, 0:1], None,
                                       ALU.mult).then_inc(edge_ready.handle, 1)
                wait_apart(pool, g, (u_ready, GB * HF * STEPS), (w0_ready, HF * STEPS), (w1_ready, HF * STEPS),
                           (edge_ready, 3 * GB * HF))
                pool.memset(a_t, 0.0).then_inc(a_cleared.handle, 1)
                for i in range(GB):
                    b = GB - 1 - i
                    wait_apart(pool, g, *(((rows_turned, 2 * HF), (filled["nt"], 8)) if i == 0 else ((w_parted, i),)))
                    pool.tensor_scalar(w_aq[:, :, b * HD:(b + 1) * HD], w_row, cf[:, C_BATCH + b:C_BATCH + b + 1],
                                       None, ALU.mult).then_inc(w_parted.handle, 1)
                for t in range(TT):
                    if t % 2 == 0:
                        pool.wait_ge(filled["ht"].handle, filled["ht"].at(g, t // 2 + 1))
                    pool.tensor_tensor(h_row[:, t, :], h_row[:, t, :], bias_row[:, :],
                                       ALU.add).then_inc(bias_added.handle, 1)

            with pool.Fori(0, G - 1) as g:
                group(g, False)
            group(G - 1, True)

        @block.tensor
        def _(pe):
            pe.wait_ge(weights_in.handle, n_weights)
            pe.matmul(psum[0][0:RANK, 0:D], lora_d, aux_d, start=True, stop=True).then_inc(lora_step.handle, 1)
            pe.wait_ge(lora_copied.handle, 1)
            pe.matmul(psum[1][0:UD, 0:D], lora_u, lora_a, start=True, stop=True).then_inc(lora_step.handle, 1)
            pe.wait_ge(lora_copied.handle, 2)
            for a in range(KT):
                pe.matmul(psum[2][:, a * D:(a + 1) * D] if KT * D <= BANK else None, lora_b[:, a * P:(a + 1) * P],
                          aux_u, start=True, stop=True).then_inc(lora_step.handle, 1)
            pe.wait_ge(lora_copied.handle, 2 + KT)

            def last_read(stage, i):
                n = AT[(stage, i)] - RING
                s, j = FILLS[n]
                assert s not in EARLY
                return drained[s], j + 1 if n >= 0 else 0

            def claim(g, stage, i, last=False):
                n = AT[(stage, i)] - RING
                while last and FILLS[n][0] in EARLY:
                    n -= RING
                s, j = FILLS[n]
                if n < 0:
                    pe.wait_ge(drained[s].handle, drained[s].before(g))
                else:
                    pe.wait_ge(drained[s].handle, drained[s].at(After(g) if s in EARLY else g, j + 1))
                return bank(stage, i)

            def early_small(ahead, get_bank):
                pe.wait_ge(x_col_in.handle, x_col_in.at(ahead, 16))
                for b in range(GB):
                    ps = get_bank("small", b)
                    for a in range(KT):
                        mm = pe.matmul(ps[0:SMALL, :], w_small[:, a, :], x_col[:, a, tokens(b)],
                                       start=a == 0, stop=a == KT - 1)
                    mm.then_inc(filled["small"].handle, 1)

            def early_decay(ahead, get_bank, part):
                if part == 0:
                    pe.wait_ge(drained["small"].handle, drained["small"].at(ahead, GB))
                for i in (2 * part, 2 * part + 1):
                    b, f = halves[i]
                    ps = get_bank("f", i)
                    pe.matmul(ps[:, :], w_second[0:HD, f * P:(f + 1) * P], small[0:HD, tokens(b)],
                              start=True, stop=True).then_inc(filled["f"].handle, 1)

            def project(g, stage, first, w):
                for i, (b, f) in enumerate(halves):
                    ps = claim(g, stage, first + i)
                    for a in range(KT):
                        mm = pe.matmul(ps[:, :], w_kqv[:, a, w, f * P:(f + 1) * P], x_col[:, a, tokens(b)],
                                       start=a == 0, stop=a == KT - 1)
                    mm.then_inc(filled[stage].handle, 1)

            def expand(g, stage, first, lo, hi):
                for i, (b, f) in enumerate(halves):
                    ps = claim(g, stage, first + i)
                    pe.matmul(ps[:, :], w_second[lo:hi, f * P:(f + 1) * P], small[lo:hi, tokens(b)],
                              start=True, stop=True).then_inc(filled[stage].handle, 1)

            def group(g, final):
                project(g, "kb", 0, 0)
                expand(g, "kb", GB * HF, 2 * HD, SMALL)
                for i, (b, f) in enumerate(halves):
                    ps = claim(g, "kss", i)
                    pe.wait_ge(k_squared.handle, k_squared.at(g, i + 1))
                    pe.matmul(ps[:, :], same_head, square_col[:, f, tokens(b)], start=True,
                              stop=True).then_inc(filled["kss"].handle, 1)
                project(g, "q", 0, 1)
                for i in range(TILES // 8):
                    wait_apart(pe, g, last_read("a", i))
                    if i % (TILES // 16) == 0:
                        f = i // (TILES // 16)
                        wait_apart(pe, g, (w0_ready, STEPS * (f + 1)), (w1_ready, STEPS * (f + 1)),
                                   (u_ready, GB * STEPS * (f + 1)), (q_ready, GB * (f + 1)))
                    ps = bank("a", i)
                    for j in range(8):
                        m = 8 * i + j
                        for h in range(HPH):
                            mm = pe.matmul(ps[quarter(h), j * 48:(j + 1) * 48], w_col[quarter(h), m, :],
                                           uq[quarter(h), m, :, :].rearrange("p b r -> p (b r)"), start=True, stop=True)
                    mm.then_inc(filled["a"].handle, 1)
                pe.wait_ge(drained["a"].handle, drained["a"].at(g, TILES // 8))
                for i in range(8):
                    ps = claim(g, "nt", i)
                    for j in range(4):
                        mm = pe.transpose(ps[:, j * P:(j + 1) * P], a_t[:, :, 4 * i + j], ident)
                    mm.then_inc(filled["nt"].handle, 1)
                project(g, "vg", 0, 2)
                expand(g, "vg", GB * HF, HD, 2 * HD)
                pe.wait_ge(solve_step.handle, solve_step.at(g, 1 + 4 * (ROWS - 1)))
                for i in range(4):
                    ps = claim(g, "tt", i)
                    for j in range(4):
                        mm = pe.transpose(ps[:, j * P:(j + 1) * P], inv[:, (4 * i + j) * P:(4 * i + j + 1) * P], ident)
                    mm.then_inc(filled["tt"].handle, 1)
                for i in range(TILES // 8):
                    inputs = ((drained["tt"], 4), (rows_turned, 3 * HF))
                    wait_apart(pe, g, last_read("xuv", i), *(inputs if i == 0 else ()))
                    ps = bank("xuv", i)
                    for j in range(8):
                        m = 8 * i + j
                        for h in range(HPH):
                            mm = pe.matmul(ps[quarter(h), j * 2 * HD:(j + 1) * 2 * HD], t_t[quarter(h), m, :],
                                           uv_row[quarter(h), :, m, :], start=True, stop=True)
                    mm.then_inc(filled["xuv"].handle, 1)

                for n in range(LEN):
                    for k in range(TEAMS):
                        turn = n * TEAMS + k + 1
                        if n == 0:
                            wait_apart(pe, g, (state_ready, 1), (xu_turned, 2 * HF), (w_parted, GB))
                            wait_apart(pe, g, (o_ready, 0))
                        else:
                            wait_apart(pe, g, (state_ready, 1 + turn - TEAMS), (o_ready, turn - TEAMS))
                        for q in team(k):
                            for f in range(HF):
                                for b in range(GB):
                                    for h in range(HPH):
                                        mm = pe.matmul(uso(k)[quarter(h), q - TP * k, f, b, :],
                                                       state[quarter(h), q, f, b, :],
                                                       uq[quarter(h), tile(f, q, n), b, :], start=True, stop=True)
                        mm.then_inc(uso_filled.handle, 1)
                    for k in range(TEAMS):
                        wait_apart(pe, g, (delta_ready, n * TEAMS + k + 1), (qs_copied, n * TEAMS + k + 1))
                        for q in team(k):
                            for f in range(HF):
                                for h in range(HPH):
                                    mm = pe.matmul(so(k)[quarter(h), q - TP * k, f, :],
                                                   delta4[quarter(h), q, f, :],
                                                   w_aq[quarter(h), tile(f, q, n), :], start=True, stop=True)
                        mm.then_inc(so_filled.handle, 1)

                def take(stage, i):
                    return claim(g, stage, i)

                if not final:
                    early_small(After(g), take)
                for i, (b, f) in enumerate(by_batch):
                    ps = claim(g, "yss", i, final)
                    if b == 0:
                        pe.wait_ge(y0_squared.handle, y0_squared.at(g, f + 1))
                    else:
                        pe.wait_ge(y1_squared.handle, y1_squared.at(g, f + 1))
                    pe.matmul(ps[:, :], same_head, r_col[:, f, tokens(b)], start=True,
                              stop=True).then_inc(filled["yss"].handle, 1)
                    if f == HF - 1 and not final:
                        early_decay(After(g), take, b)
                for i in range(TT // 2):
                    ps = claim(g, "wo", i, final)
                    pe.wait_ge(y_normed.handle, y_normed.at(g, HF * (2 * i * P // NT + 1)))
                    for j in range(2):
                        t = 2 * i + j
                        for f in range(HF):
                            mm = pe.matmul(ps[:, j * D:(j + 1) * D], y_col[:, f, t * P:(t + 1) * P], w_out[:, f, :],
                                           start=f == 0, stop=f == HF - 1)
                    mm.then_inc(filled["wo"].handle, 1)
                for i in range(TT // 2):
                    ps = claim(g, "ht", i, final)
                    pe.wait_ge(h_normed.handle, h_normed.at(g, 2 * i + 2))
                    for a in range(KT):
                        for j in range(2):
                            at = (a * 2 + j) * P
                            mm = pe.transpose(ps[:, at:at + P], h_row[:, 2 * i + j, a * P:(a + 1) * P], ident)
                    mm.then_inc(filled["ht"].handle, 1)
                for i in range(TT // 2):
                    ps = claim(g, "ff", i, final)
                    pe.wait_ge(drained["ht"].handle, drained["ht"].at(g, i + 1))
                    for j in range(2):
                        t = 2 * i + j
                        for a in range(KT):
                            mm = pe.matmul(ps[:, j * D:(j + 1) * D], h_col[:, a, t * P:(t + 1) * P], w_ffn[:, a, :],
                                           start=a == 0, stop=a == KT - 1)
                    mm.then_inc(filled["ff"].handle, 1)

            early_small(After(-1), bank)
            for part in range(2):
                early_decay(After(-1), bank, part)
            pe.wait_ge(drained["small"].handle, drained["small"].at(0, GB))
            pe.wait_ge(drained["f"].handle, drained["f"].at(0, GB * HF))
            with pe.Fori(0, G - 1) as g:
                group(g, False)
            group(G - 1, True)

        @block.scalar
        def _(act):
            act.wait_ge(weights_in.handle, n_weights)
            act.wait_ge(set_up.handle, 5)
            eps2 = cf[:, C_EPS:C_EPS + 1]
            eps_ln = cf[:, C_EPS + 1:C_EPS + 2]
            def early_copies(ahead):
                for b in range(GB):
                    act.wait_ge(filled["small"].handle, filled["small"].at(ahead, b + 1))
                    act.activation(small[0:SMALL, tokens(b)], bank("small", b)[0:SMALL, :],
                                   ACT.Copy).then_inc(drained["small"].handle, 1)

            def early_sigmoids(ahead):
                for i, (b, f) in enumerate(halves):
                    act.wait_ge(filled["f"].handle, filled["f"].at(ahead, i + 1))
                    act.activation(logf[:, f, b, :, 1:SLOTS], bank("f", i)[:, :].rearrange("p (n t) -> p n t", t=TB),
                                   ACT.Sigmoid).then_inc(drained["f"].handle, 1)

            def early_logs(ahead):
                for i, (b, f) in enumerate(halves):
                    act.wait_ge(f_floored.handle, f_floored.at(ahead, i + 1))
                    act.activation(logf[:, f, b, :, 1:SLOTS], logf[:, f, b, :, 1:SLOTS],
                                   ACT.Ln).then_inc(f_logged.handle, 1)

            def group(g, final):
                act.wait_ge(filled["ff"].handle, filled["ff"].before(g))
                for i, (b, f) in enumerate(halves):
                    act.wait_ge(filled["kb"].handle, filled["kb"].at(g, i + 1))
                    act.activation(k_col[:, f, tokens(b)], bank("kb", i)[:, :],
                                   ACT.Silu).then_inc(drained["kb"].handle, 1)
                for i, (b, f) in enumerate(halves):
                    act.wait_ge(filled["kb"].handle, filled["kb"].at(g, GB * HF + i + 1))
                    act.activation(beta_col[:, f, tokens(b)], bank("kb", GB * HF + i)[:, :],
                                   ACT.Sigmoid).then_inc(drained["kb"].handle, 1)
                act.preload_act_table_set("natural_log_exp_and_others")
                act.wait_ge(out_stored.handle, out_stored.before(g))
                for i, (b, f) in enumerate(halves):
                    act.wait_ge(filled["kss"].handle, filled["kss"].at(g, i + 1))
                    act.activation(ss_col[:, f, tokens(b)], bank("kss", i)[:, :], ACT.Ln,
                                   bias=eps2).then_inc(drained["kss"].handle, 1)
                    act.wait_ge(drained["kss"].handle, drained["kss"].at(g, i + 1))
                    act.activation(ss_col[:, f, tokens(b)], ss_col[:, f, tokens(b)], ACT.Exp,
                                   scale=-0.5).then_inc(r_ready.handle, 1)
                for f in range(HF):
                    act.wait_ge(centred.handle, centred.at(g, GB * (f + 1)))
                    act.activation(ep[:, f, :, :, :], centre[:, f, :, :, :], ACT.Exp).then_inc(ep_ready.handle, 1)
                    act.activation(em[:, f, :, :, :], centre[:, f, :, :, :], ACT.Exp,
                                   scale=-1.0).then_inc(em_ready.handle, 1)
                for i, (b, f) in enumerate(halves):
                    act.wait_ge(filled["q"].handle, filled["q"].at(g, i + 1))
                    act.activation(q_col[:, f, tokens(b)], bank("q", i)[:, :],
                                   ACT.Silu).then_inc(drained["q"].handle, 1)
                low5 = low.rearrange("p (i h b j) -> p i h b j", h=HPH, b=GB, i=ROWS)
                act.wait_ge(u_ready.handle, u_ready.at(g, GB * HF * STEPS))
                for i in range(8):
                    b, r = i // 4, 4 * (i % 4)
                    act.wait_ge(filled["nt"].handle, filled["nt"].at(g, i + 1))
                    src = bank("nt", i)[:, :].rearrange("p (i h b j) -> p i h b j", i=4, h=HPH, b=GB)[:, :, :, b, :]
                    act.activation(low5[:, r:r + 4, :, b, :], src,
                                   ACT.Copy).then_inc(drained["nt"].handle, 1)
                for i, (b, f) in enumerate(halves):
                    act.wait_ge(filled["vg"].handle, filled["vg"].at(g, i + 1))
                    act.activation(v_col[:, tiles(f), b * ROWS + 1:(b + 1) * ROWS:STEPS],
                                   bank("vg", i)[:, :].rearrange("p (n t) -> p n t", t=TB),
                                   ACT.Silu).then_inc(drained["vg"].handle, 1)
                for i, (b, f) in enumerate(halves):
                    act.wait_ge(filled["vg"].handle, filled["vg"].at(g, GB * HF + i + 1))
                    act.activation(gate[:, f, tokens(b)], bank("vg", GB * HF + i)[:, :],
                                   ACT.Sigmoid).then_inc(drained["vg"].handle, 1)
                act.wait_ge(rows_turned.handle, rows_turned.at(g, 2 * HF))
                act.wait_ge(filled["a"].handle, filled["a"].at(g, TILES // 8))
                for i in range(4):
                    act.wait_ge(filled["tt"].handle, filled["tt"].at(g, i + 1))
                    src = bank("tt", i)[:, :].rearrange("p (i m) -> p i m", i=4)
                    for b in range(GB):
                        r = b * ROWS + 4 * i
                        last = act.activation(t_t[:, :, r:r + 4].rearrange("p m i -> p i m"), src, ACT.Copy,
                                              scale=cf[:, C_BATCH + b:C_BATCH + b + 1])
                    last.then_inc(drained["tt"].handle, 1)
                for i in range(TILES // 8):
                    act.wait_ge(filled["xuv"].handle, filled["xuv"].at(g, i + 1))
                    act.activation(uv_row[:, :, 8 * i:8 * (i + 1), :],
                                   bank("xuv", i)[:, :].rearrange("p (m w c) -> p w m c", w=2, c=HD),
                                   ACT.Copy).then_inc(drained["xuv"].handle, 1)
                act.preload_act_table_set("natural_log_exp_and_others")
                for n in range(LEN):
                    for k in range(TEAMS):
                        turn = n * TEAMS + k + 1
                        if n > 0:
                            act.wait_ge(o_ready.handle, o_ready.at(g, turn - TEAMS))
                        act.wait_ge(us_turned.handle, us_turned.at(g, turn))
                        act.activation(qs[:, k * TP:(k + 1) * TP, :, :, :].rearrange("p q f b t -> p (q f b) t"),
                                       uso(k)[:, :, :, :, ROWS:RQ].rearrange("p q f b t -> p (q f b) t"),
                                       ACT.Copy).then_inc(qs_copied.handle, 1)
                if not final:
                    early_copies(After(g))
                for i, (b, f) in enumerate(by_batch):
                    act.wait_ge(filled["yss"].handle, filled["yss"].at(g, i + 1))
                    act.activation(r_col[:, f, tokens(b)], bank("yss", i)[:, :], ACT.Ln, scale=1.0 / HD,
                                   bias=eps2).then_inc(drained["yss"].handle, 1)
                    act.wait_ge(drained["yss"].handle, drained["yss"].at(g, i + 1))
                    act.activation(r_col[:, f, tokens(b)], r_col[:, f, tokens(b)], ACT.Exp,
                                   scale=-0.5).then_inc(yr_ready.handle, 1)
                    if b == 0:
                        act.wait_ge(y_ready.handle, y_ready.at(g, HF + f + 1))
                        act.activation(r_col[:, f, tokens(1)], y_col[:, f, tokens(1)],
                                       ACT.Square).then_inc(y1_squared.handle, 1)
                if not final:
                    early_sigmoids(After(g))
                act.preload_act_table(ACT.Sqrt)
                for ln in range(2):
                    for c in range(2):
                        some = slice(c * TT // 2, (c + 1) * TT // 2)
                        act.wait_ge(mean_ready.handle, mean_ready.at(g, ln * TT + (c + 1) * TT // 2))
                        act.activation(rstd[:, some], mean_var[:, some, 1], ACT.Sqrt,
                                       bias=eps_ln).then_inc(std_ready.handle, 1)
                        if ln == 1:
                            continue
                        for i in range(c * TT // 4, (c + 1) * TT // 4):
                            act.wait_ge(filled["ht"].handle, filled["ht"].at(g, i + 1))
                            act.activation(h_col[:, :, 2 * i * P:2 * (i + 1) * P],
                                           bank("ht", i)[:, :].rearrange("p (a t) -> p a t", a=KT),
                                           ACT.Copy).then_inc(drained["ht"].handle, 1)
                    if ln == 0 and not final:
                        early_logs(After(g))
                act.preload_act_table(ACT.Silu)

            early_copies(After(-1))
            early_sigmoids(After(-1))
            early_logs(After(-1))
            act.preload_act_table(ACT.Silu)
            with act.Fori(0, G - 1) as g:
                group(g, False)
            group(G - 1, True)

        @block.vector
        def _(dve):
            dve.wait_ge(weights_in.handle, n_weights)
            dve.wait_ge(lora_step.handle, 1)
            dve.tensor_copy(lora_a, psum[0][0:RANK, 0:D]).then_inc(lora_copied.handle, 1)
            dve.wait_ge(lora_step.handle, 2)
            dve.tensor_copy(lora_b, psum[1][0:UD, 0:D]).then_inc(lora_copied.handle, 1)
            dve.wait_ge(lora_step.handle, 2 + KT)
            for a in range(KT):
                dve.tensor_tensor(w_ffn[:, a, :], w_ffn[:, a, :], psum[2][:, a * D:(a + 1) * D],
                                  ALU.add).then_inc(lora_copied.handle, 1)
            dve.wait_ge(set_up.handle, 5)
            def early_carry(ahead):
                carry3 = carry.rearrange("p (n s) -> p n s", s=SLOTS)
                dve.memset(carry3, 1.0).then_inc(carry_set.handle, 1)
                wait_apart(dve, ahead, (carry_set, 1))
                dve.memset(carry3[:, :, 0:1], 0.0).then_inc(carry_set.handle, 1)
                dve.wait_ge(carry_set.handle, carry_set.at(ahead, 2))

            def early_floors(ahead):
                for i, (b, f) in enumerate(halves):
                    dve.wait_ge(drained["f"].handle, drained["f"].at(ahead, i + 1))
                    dve.tensor_scalar(logf[:, f, b, :, 1:SLOTS], logf[:, f, b, :, 1:SLOTS], MIN_DECAY, None,
                                      ALU.max).then_inc(f_floored.handle, 1)

            def group(g, final):
                for i, (b, f) in enumerate(halves):
                    dve.wait_ge(drained["kb"].handle, drained["kb"].at(g, i + 1))
                    dve.tensor_tensor(square_col[:, f, tokens(b)], k_col[:, f, tokens(b)], k_col[:, f, tokens(b)],
                                      ALU.mult).then_inc(k_squared.handle, 1)
                for f in range(HF):
                    dve.wait_ge(f_logged.handle, f_logged.at(g, GB * (f + 1)))
                    dve.tensor_tensor_scan(dd4[:, f, :, :, :].rearrange("p b n s -> p (b n s)"), carry,
                                           logf[:, f, :, :, :].rearrange("p b n s -> p (b n s)"),
                                           0.0, ALU.mult, ALU.add).then_inc(summed.handle, 1)
                    dve.wait_ge(summed.handle, summed.at(g, f + 1))
                    for b in range(GB):
                        mid = dd4[:, f, b, :, TB // 2:TB // 2 + 1].to_broadcast([P, NBLK, SLOTS])
                        dve.tensor_tensor(centre[:, f, b, :, :], dd4[:, f, b, :, :], mid,
                                          ALU.subtract).then_inc(centred.handle, 1)
                for f in range(HF):
                    for b in range(GB):
                        i = halves.index((b, f))
                        dve.wait_ge(r_ready.handle, r_ready.at(g, i + 1))
                        dve.tensor_tensor(k_col[:, f, tokens(b)], k_col[:, f, tokens(b)], ss_col[:, f, tokens(b)],
                                          ALU.mult).then_inc(k_normed.handle, 1)
                    for b in range(GB):
                        i = halves.index((b, f))
                        dve.wait_ge(k_normed.handle, k_normed.at(g, i + 1))
                        dve.wait_ge(drained["kb"].handle, drained["kb"].at(g, GB * HF + i + 1))
                        dve.scalar_tensor_tensor(beta_col[:, f, tokens(b)], beta_col[:, f, tokens(b)], 2.0,
                                                 k_col[:, f, tokens(b)], ALU.mult,
                                                 ALU.mult).then_inc(kb_ready.handle, 1)
                    for b in range(GB):
                        dve.wait_ge(kb_ready.handle, kb_ready.at(g, halves.index((b, f)) + 1))
                        dve.wait_ge(ep_ready.handle, ep_ready.at(g, f + 1))
                        for s in range(STEPS):
                            dve.tensor_tensor(uq[:, tiles(f), b, s:ROWS:STEPS], blocks(beta_col, b, f),
                                              ep[:, f, b, :, s:s + TB], ALU.mult).then_inc(u_ready.handle, 1)
                    dve.wait_ge(em_ready.handle, em_ready.at(g, f + 1))
                    w_half(dve, 0, f, w0_ready)
                for i in range(TILES // 8):
                    wait_apart(dve, g, (filled["a"], i + 1), (a_cleared, 1))
                    ps = bank("a", i)[:, 0:8 * GB * RQ].rearrange("p (m b r) -> p m b r", m=8, b=GB)
                    own = slice(8 * i, 8 * (i + 1))
                    for to, mask, src in ((a_t, ci[:, M_LOW:M_Q], ps[:, :, :, 0:ROWS]),
                                          (aq, ci[:, M_Q:M_END], ps[:, :, :, ROWS:RQ])):
                        last = dve.copy_predicated(
                            to[:, own, :].rearrange("p m (b r) -> p m b r", b=GB),
                            mask.rearrange("p (b r) -> p b r", b=GB).unsqueeze(1).to_broadcast(list(src.shape)), src)
                    last.then_inc(drained["a"].handle, 1)
                    if i == 0:
                        dve.wait_ge(w1_ready.handle, w1_ready.at(g, HF * STEPS))
                        dve.wait_ge(q_ready.handle, q_ready.at(g, GB * HF))
                        dve.wait_ge(edge_ready.handle, edge_ready.at(g, 3 * GB * HF))
                    if i % 2 == 0 and i < 4 * HF:
                        f = i // 4
                        if i % 4 == 0:
                            dve.wait_ge(u_ready.handle, u_ready.at(g, GB * HF * STEPS))
                            dve.transpose(u_row[:, tiles(f), :], uq[:, tiles(f), :, 0:ROWS]).then_inc(rows_turned.handle, 1)
                        else:
                            dve.wait_ge(w0_ready.handle, w0_ready.at(g, HF * STEPS))
                            dve.transpose(w_row[:, tiles(f), :], w_col[:, tiles(f), :]).then_inc(rows_turned.handle, 1)
                inv4 = inv.rearrange("p (i k j) -> p i k j", i=ROWS, j=ROWS)
                low4 = low.rearrange("p (i k j) -> p i k j", i=ROWS, j=ROWS)
                eye = cf[:, C_EYE:C_EYE + ROWS * ROWS].rearrange("p (i j) -> p i j", i=ROWS)
                dve.tensor_copy(inv4, eye.unsqueeze(2).to_broadcast([P, ROWS, GB * HPH, ROWS])).then_inc(solve_step.handle, 1)
                dve.wait_ge(drained["nt"].handle, drained["nt"].at(g, 8))
                for p in range(ROWS - 1):
                    below, width = ROWS - 1 - p, p + 1
                    size = [P, below, GB * HPH // 2, width]
                    words = below * GB * HPH // 2 * width
                    for c in range(2):
                        ks = slice(c * GB * HPH // 2, (c + 1) * GB * HPH // 2)
                        own = prod[:, c * prod.shape[1] // 2:(c + 1) * prod.shape[1] // 2]
                        step = own[:, 0:words].rearrange("p (r k c) -> p r k c", r=below, c=width)
                        dve.wait_ge(solve_step.handle, solve_step.at(g, max(1, 4 * p + c)))
                        dve.tensor_tensor(step, low4[:, p + 1:ROWS, ks, p:p + 1].to_broadcast(size),
                                          inv4[:, p:p + 1, ks, 0:width].to_broadcast(size),
                                          ALU.mult).then_inc(solve_step.handle, 1)
                    for c in range(2):
                        ks = slice(c * GB * HPH // 2, (c + 1) * GB * HPH // 2)
                        own = prod[:, c * prod.shape[1] // 2:(c + 1) * prod.shape[1] // 2]
                        step = own[:, 0:words].rearrange("p (r k c) -> p r k c", r=below, c=width)
                        dve.wait_ge(solve_step.handle, solve_step.at(g, 4 * p + 2 + c))
                        dve.tensor_tensor(inv4[:, p + 1:ROWS, ks, 0:width], inv4[:, p + 1:ROWS, ks, 0:width], step,
                                          ALU.subtract).then_inc(solve_step.handle, 1)
                dve.wait_ge(filled["vg"].handle, filled["vg"].at(g, 2 * GB * HF))
                for f in range(HF):
                    dve.wait_ge(drained["vg"].handle, drained["vg"].at(g, GB * (f + 1)))
                    dve.transpose(v_row[:, tiles(f), :], v_col[:, tiles(f), :]).then_inc(rows_turned.handle, 1)
                dve.wait_ge(edge_ready.handle, edge_ready.at(g, 3 * GB * HF))
                flat_state = state[:, :, :, :, :].rearrange("p q f b v -> p (q f b) v")
                dve.tensor_tensor(flat_state, flat_state,
                                  enter[:, :, :, :].rearrange("p q f b -> p (q f b)").unsqueeze(2).to_broadcast(
                                      [P, PAIRS * HF * GB, HD]),
                                  ALU.mult).then_inc(state_ready.handle, 1)
                for i in range(2 * HF):
                    some = slice(i * TILES // 4, (i + 1) * TILES // 4)
                    dve.wait_ge(drained["xuv"].handle, drained["xuv"].at(g, (i + 1) * TILES // 32))
                    dve.transpose(uq[:, some, :, 0:ROWS], u_row[:, some, :]).then_inc(xu_turned.handle, 1)
                tv = v_row.rearrange("p (f q n) v -> p n q f v", f=HF, q=PAIRS)
                outputs = o_col[:, :, :].rearrange("p f (b q n t) -> p f n q b t", b=GB, q=PAIRS, t=TB)

                def mine(tensor, k):
                    width = tensor.shape[1] // TEAMS
                    return tensor[:, k * width:(k + 1) * width]

                states = state[:, :, :, :, :].rearrange("p q f b v -> p (q f b v)")
                for n in range(LEN):
                    for k in range(TEAMS):
                        turn = n * TEAMS + k + 1
                        dve.wait_ge(uso_filled.handle, uso_filled.at(g, turn))
                        dve.transpose(mine(us_row, k),
                                      uso(k)[:, :, :, :, 0:ROWS]).then_inc(us_turned.handle, 1)
                        dve.wait_ge(us_turned.handle, us_turned.at(g, turn))
                        dve.tensor_tensor(mine(delta, k).rearrange("p (q f v) -> p q f v", q=TP, f=HF),
                                          tv[:, n, k * TP:(k + 1) * TP, :, :],
                                          mine(us_row, k).rearrange("p (q f v) -> p q f v", q=TP, f=HF),
                                          ALU.subtract).then_inc(delta_ready.handle, 1)
                    for k in range(TEAMS):
                        turn = n * TEAMS + k + 1
                        dve.wait_ge(so_filled.handle, so_filled.at(g, turn))
                        dve.transpose(mine(turned, k).rearrange("p (m c) -> p m c", c=GB * HD),
                                      so(k)[:, :, :, 0:GB * HD].rearrange("p q f c -> p (q f) c")
                                      ).then_inc(s_turned.handle, 1)
                        dve.wait_ge(s_turned.handle, s_turned.at(g, turn))
                        dve.tensor_tensor(mine(moved, k), mine(states, k), mine(turned, k),
                                          ALU.add).then_inc(moved_ready.handle, 1)
                        dve.wait_ge(moved_ready.handle, moved_ready.at(g, turn))
                        decay = edge[:, n, k * TP:(k + 1) * TP, :, :].rearrange("p q f b -> p (q f b)").unsqueeze(2)
                        dve.tensor_tensor(mine(states, k).rearrange("p (s v) -> p s v", v=HD),
                                          mine(moved, k).rearrange("p (s v) -> p s v", v=HD),
                                          decay.to_broadcast([P, TP * HF * GB, HD]),
                                          ALU.mult).then_inc(state_ready.handle, 1)
                        for f in range(HF):
                            last = dve.tensor_tensor(
                                outputs[:, f, n, k * TP:(k + 1) * TP, :, :], qs[:, k * TP:(k + 1) * TP, f, :, :],
                                so(k)[:, :, f, GB * HD:].rearrange("p q (b t) -> p q b t", b=GB), ALU.add)
                        last.then_inc(o_ready.handle, 1)
                dve.wait_ge(o_ready.handle, o_ready.at(g, TURNS))
                for i, (b, f) in enumerate(by_batch):
                    dve.tensor_tensor(y_col[:, f, tokens(b)], o_col[:, f, tokens(b)], gate[:, f, tokens(b)],
                                      ALU.mult).then_inc(y_ready.handle, 1)
                    if b == 0:
                        dve.wait_ge(y_ready.handle, y_ready.at(g, i + 1))
                        dve.tensor_tensor(r_col[:, f, tokens(b)], y_col[:, f, tokens(b)], y_col[:, f, tokens(b)],
                                          ALU.mult).then_inc(y0_squared.handle, 1)
                for i, (b, f) in enumerate(by_batch):
                    dve.wait_ge(yr_ready.handle, yr_ready.at(g, i + 1))
                    dve.scalar_tensor_tensor(y_col[:, f, tokens(b)], y_col[:, f, tokens(b)], norm_col[:, f:f + 1],
                                             r_col[:, f, tokens(b)], ALU.mult, ALU.mult).then_inc(y_normed.handle, 1)
                if not final:
                    early_carry(After(g))
                dve.wait_ge(x_row_in.handle, x_row_in.at(g, 16))
                for ln in range(2):
                    stage = "wo" if ln == 0 else "ff"
                    if ln == 1 and not final:
                        early_floors(After(g))
                    for c in range(2):
                        some = range(c * TT // 2, (c + 1) * TT // 2)
                        for i in range(some[0] // 2, some[-1] // 2 + 1):
                            if ln == 1:
                                dve.wait_ge(bias_added.handle, bias_added.at(g, 2 * i + 2))
                            dve.wait_ge(filled[stage].handle, filled[stage].at(g, i + 1))
                            dve.tensor_tensor(h_row[:, 2 * i:2 * i + 2, :], h_row[:, 2 * i:2 * i + 2, :],
                                              bank(stage, i)[:, :].rearrange("p (t c) -> p t c", c=D),
                                              ALU.add).then_inc(drained[stage].handle, 1)
                        for t in some:
                            dve.wait_ge(drained[stage].handle, drained[stage].at(g, t // 2 + 1))
                            dve.bn_stats(stats[:, t, :], h_row[:, t, :]).then_inc(stats_ready.handle, 1)
                        for t in some:
                            wait_apart(dve, g, (stats_ready, ln * TT + t + 1))
                            dve.bn_aggr(mean_var[:, t, :], stats[:, t, :]).then_inc(mean_ready.handle, 1)
                        dve.wait_ge(std_ready.handle, std_ready.at(g, 2 * ln + c + 1))
                        dve.reciprocal(rstd[:, some[0]:some[-1] + 1],
                                       rstd[:, some[0]:some[-1] + 1]).then_inc(rstd_ready.handle, 1)
                        dve.wait_ge(rstd_ready.handle, rstd_ready.at(g, 2 * ln + c + 1))
                        for t in some:
                            dve.tensor_scalar(h_row[:, t, :], h_row[:, t, :], mean_var[:, t, 0:1], rstd[:, t:t + 1],
                                              ALU.subtract, ALU.mult).then_inc(h_normed.handle, 1)

            early_carry(After(-1))
            early_floors(After(-1))
            with dve.Fori(0, G - 1) as g:
                group(g, False)
            group(G - 1, True)


_ARGS = ["x", "xt", "Wq", "Wk", "Wv", "Wf1", "Wf2", "Wbeta", "Wog1", "Wog2", "norm_w", "Wo", "ffn_wt", "ffn_b",
         "lora_down_t", "lora_up_t", "down_aux", "up_aux_t", "const_f", "const_i",
         "const_keep"]


def kernel(**inputs):
    import concourse.bacc as _bacc
    from concourse import mybir as _mybir
    from concourse.bass_utils import run_bass_kernel_spmd as _run

    a = {k: np.asarray(v) for k, v in inputs.items()}
    x = a["L0_attn_x"]
    batches, length, width = x.shape
    segments = length // SEG
    grid = (batches // (GB * PAIRS), GB * PAIRS, segments, SEG, width)
    grouped = x.reshape(grid).transpose(0, 2, 1, 3, 4).reshape(-1, GB * PAIRS * SEG, width)
    laid = {"x": grouped, "xt": grouped.reshape(-1, width).T,
            "ffn_wt": a["L0_ffn_W"].T, "ffn_b": a["L0_ffn_b"],
            "lora_down_t": a["L0_ffn_lora_down"].T, "lora_up_t": a["L0_ffn_lora_up"].T,
            "down_aux": a["L0_ffn_down_aux"], "up_aux_t": a["L0_ffn_up_aux"].T}
    for name in ("Wq", "Wk", "Wv", "Wf1", "Wf2", "Wbeta", "Wog1", "Wog2", "Wo"):
        laid[name] = a["L0_attn_" + name]
    laid["norm_w"] = a["L0_attn_norm_w"].reshape(HF, P).T
    laid["const_f"], laid["const_i"] = constants()
    laid["const_keep"] = np.broadcast_to((np.arange(len(grouped)) % segments != 0).astype(np.float32)[:, None],
                                         (len(grouped), P))

    nc = _bacc.Bacc("TRN2", target_bir_lowering=False, num_devices=1)
    arrays, args = {}, []
    for name in _ARGS:
        v = np.ascontiguousarray(laid[name])
        arrays[f"in_{name}_dram"] = v
        args.append(nc.dram_tensor(f"in_{name}_dram", v.shape, _mybir.dt.from_np(v.dtype), kind="ExternalInput").ap())
    args.append(nc.dram_tensor("out_0_dram", grouped.shape, _mybir.dt.from_np(x.dtype), kind="ExternalOutput").ap())
    delta_block(nc, *args)
    r = _run(nc, [arrays], core_ids=[0])
    o = np.asarray(r.results[0]["out_0_dram"]).reshape(grid[0], segments, GB * PAIRS, SEG, width)
    return o.transpose(0, 2, 1, 3, 4).reshape(x.shape)
```
